# Optimizing a Trainium2 kernel written in Bass

```python
import numpy as np
import jax
import jax.numpy as jnp

def _softmax(x, axis=-1):
    return jax.nn.softmax(x, axis=axis)

def _gelu(x):
    return jax.nn.gelu(x, approximate=True)

def _silu(x):
    return jax.nn.silu(x)

def _sigmoid(x):
    return jax.nn.sigmoid(x)

def _layernorm(x, axis=-1, eps=1e-05):
    m = jnp.mean(x, axis=axis, keepdims=True)
    v = jnp.var(x, axis=axis, keepdims=True)
    return (x - m) / jnp.sqrt(v + eps)

def _scatter_add(tgt, idx, src, axis=0):
    return tgt.at[idx].add(src)

def _segment_sum(src, seg, n):
    return jax.ops.segment_sum(src, seg, n)
kernel_name = 'mk_decoder_preln_d1_seqx_r8_409993'

def setup_inputs(seed: int=0):
    np.random.seed(seed)
    _w = jnp.asarray

    def _rec_inputs():
        import jax
        import jax.numpy as jnp
        _rk = jax.random.key(seed)
        x = 7.22e-05 + 1 * jax.random.normal(jax.random.fold_in(_rk, 1), (8, 128, 512), jnp.float32)
        _lenS = 128 - jax.random.randint(jax.random.fold_in(_rk, 7), (8,), 0, max(1, 128 // 4) + 1, jnp.int32)
        _lenS2 = 128 - jax.random.randint(jax.random.fold_in(_rk, 8), (8,), 0, max(1, 128 // 4) + 1, jnp.int32)
        _ctx_4096P = jax.random.normal(jax.random.fold_in(_rk, 11), (8, 16, 512), jnp.float32)
        _ctx_4096c = jax.random.dirichlet(jax.random.fold_in(_rk, 511), 0.3 * jnp.ones((16,), jnp.float32), (8, 128))
        _ctx_4096t = jnp.einsum('bsk,bkd->bsd', _ctx_4096c, _ctx_4096P)
        _ctx_4096t = _ctx_4096t * jax.lax.rsqrt(jnp.mean(jnp.square(_ctx_4096t)) + 1e-12) * 0.953939
        ctx_4096 = 4.13588e-05 + 0.999923 * (_ctx_4096t + 0.3 * jax.random.normal(jax.random.fold_in(_rk, 611), (8, 128, 512), jnp.float32))
        _validS = jnp.arange(128)[None, :] < _lenS[:, None]
        _validS2 = jnp.arange(128)[None, :] < _lenS2[:, None]
        _causal = jnp.tril(jnp.ones((128, 128), dtype=bool))
        mask_BxSxS2_bk0 = jnp.logical_not(jnp.broadcast_to(_validS2[:, None, :], (8, 128, 128)))
        return (x, ctx_4096, mask_BxSxS2_bk0)
    x, ctx_4096, mask_BxSxS2_bk0 = _rec_inputs()

    def _L0_attn_setup():
        import jax, jax.numpy as jnp
        import numpy as np
        H = 512
        D = H // 4
        key = jax.random.key(seed)
        k1, k2, k3, k4, k5 = jax.random.split(key, 5)
        x = jax.random.normal(k1, (4, 512, H), dtype=jnp.float32)
        s_in = 1.0 / np.sqrt(H)
        Wqkv = jax.random.normal(k2, (H, 3 * D), dtype=jnp.float32) * s_in
        bqkv = jax.random.normal(k3, (3 * D,), dtype=jnp.float32) * 0.01
        Wo = jax.random.normal(k4, (D, H), dtype=jnp.float32) * (1.0 / np.sqrt(D))
        bo = jax.random.normal(k5, (H,), dtype=jnp.float32) * 0.01
        return {'x': x, 'Wqkv': Wqkv, 'bqkv': bqkv, 'Wo': Wo, 'bo': bo}
    _L0_attn_all = _L0_attn_setup()
    _L0_attn_in = {k: v for k, v in _L0_attn_all.items() if k in ('Wqkv', 'bqkv', 'Wo', 'bo')}
    del _L0_attn_all

    def _L0_xattn_setup():
        import jax, jax.numpy as jnp
        import numpy as np
        B, LQ, LK, D, H, DH = (2, 128, 128, 512, 32, 128)
        EPS = 1e-05

        def _rmsnorm(x, weight):
            var = jnp.mean(jnp.square(x), axis=-1, keepdims=True)
            return x * jax.lax.rsqrt(var + EPS) * weight
        key = jax.random.key(seed)
        ks = jax.random.split(key, 8)
        scale = 0.02
        return {'hidden_states': jax.random.normal(ks[0], (B, LQ, D), jnp.float32), 'key_value_states': jax.random.normal(ks[1], (B, LK, D), jnp.float32), 'attention_mask': jax.random.randint(ks[2], (B, LQ, LK), 0, 2) > 0, 'position_bias': jax.random.normal(ks[3], (H, LQ, LK), jnp.float32), 'ln_weight': jnp.ones((D,), jnp.float32), 'w_q': jax.random.normal(ks[4], (H * DH, D), jnp.float32) * scale, 'w_k': jax.random.normal(ks[5], (H * DH, D), jnp.float32) * scale, 'w_v': jax.random.normal(ks[6], (H * DH, D), jnp.float32) * scale, 'w_out': jax.random.normal(ks[7], (D, H * DH), jnp.float32) * scale}
    _L0_xattn_all = _L0_xattn_setup()
    _L0_xattn_in = {k: v for k, v in _L0_xattn_all.items() if k in ('position_bias', 'ln_weight', 'w_q', 'w_k', 'w_v', 'w_out')}
    del _L0_xattn_all

    def _L0_ffn_setup():
        import jax, jax.numpy as jnp
        import numpy as np
        R = 16
        ALPHA = 32
        SCALING = ALPHA / R
        E = 8
        TOP_K = 2
        key = jax.random.key(seed)
        ks = jax.random.split(key, 5)
        B, S, D = (4, 256, 512)
        x = jax.random.normal(ks[0], (B, S, D), dtype=jnp.float32)
        base_W = jax.random.normal(ks[1], (D, D), dtype=jnp.float32) * 0.02
        router_W = jax.random.normal(ks[2], (E, D), dtype=jnp.float32) * 0.02
        lora_A = jax.random.normal(ks[3], (E, D, R), dtype=jnp.float32) * 0.02
        lora_B = jax.random.normal(ks[4], (E, R, D), dtype=jnp.float32) * 0.02
        return {'x': x, 'base_W': base_W, 'router_W': router_W, 'lora_A': lora_A, 'lora_B': lora_B}
    _L0_ffn_all = _L0_ffn_setup()
    _L0_ffn_in = {k: v for k, v in _L0_ffn_all.items() if k in ('base_W', 'router_W', 'lora_A', 'lora_B')}
    del _L0_ffn_all
    return {'x': x, 'ctx_4096': ctx_4096, 'mask_BxSxS2_bk0': mask_BxSxS2_bk0, 'L0_attn_Wqkv': _L0_attn_in['Wqkv'], 'L0_attn_bqkv': _L0_attn_in['bqkv'], 'L0_attn_Wo': _L0_attn_in['Wo'], 'L0_attn_bo': _L0_attn_in['bo'], 'L0_xattn_position_bias': _L0_xattn_in['position_bias'], 'L0_xattn_ln_weight': _L0_xattn_in['ln_weight'], 'L0_xattn_w_q': _L0_xattn_in['w_q'], 'L0_xattn_w_k': _L0_xattn_in['w_k'], 'L0_xattn_w_v': _L0_xattn_in['w_v'], 'L0_xattn_w_out': _L0_xattn_in['w_out'], 'L0_ffn_base_W': _L0_ffn_in['base_W'], 'L0_ffn_router_W': _L0_ffn_in['router_W'], 'L0_ffn_lora_A': _L0_ffn_in['lora_A'], 'L0_ffn_lora_B': _L0_ffn_in['lora_B']}

def reference(x, ctx_4096, mask_BxSxS2_bk0, L0_attn_Wqkv, L0_attn_bqkv, L0_attn_Wo, L0_attn_bo, L0_xattn_position_bias, L0_xattn_ln_weight, L0_xattn_w_q, L0_xattn_w_k, L0_xattn_w_v, L0_xattn_w_out, L0_ffn_base_W, L0_ffn_router_W, L0_ffn_lora_A, L0_ffn_lora_B):
    import jax
    import jax.numpy as jnp

    def _L0_attn_ref(x, Wqkv, bqkv, Wo, bo):
        import jax, jax.numpy as jnp
        import numpy as np
        H = 512
        D = H // 4
        B, S, C = x.shape
        d = C // 4
        qkv = jnp.einsum('bsc,cf->bsf', x, Wqkv) + bqkv
        qkv = qkv.reshape(B, S, 3, d)
        q, k, v = (qkv[:, :, 0], qkv[:, :, 1], qkv[:, :, 2])
        scale = 1.0 / jnp.sqrt(jnp.float32(d)).astype(x.dtype)
        attn = jnp.einsum('bqd,bkd->bqk', q, k) * scale
        attn = jax.nn.softmax(attn, axis=-1)
        out = jnp.einsum('bqk,bkd->bqd', attn, v)
        return jnp.einsum('bqd,dc->bqc', out, Wo) + bo

    def _L0_xattn_ref(hidden_states, key_value_states, attention_mask, position_bias, ln_weight, w_q, w_k, w_v, w_out):
        import jax, jax.numpy as jnp
        import numpy as np
        B, LQ, LK, D, H, DH = (2, 128, 128, 512, 32, 128)
        EPS = 1e-05

        def _rmsnorm(x, weight):
            var = jnp.mean(jnp.square(x), axis=-1, keepdims=True)
            return x * jax.lax.rsqrt(var + EPS) * weight
        x = _rmsnorm(hidden_states, ln_weight)
        b, lq, _ = x.shape
        lk = key_value_states.shape[1]
        h_q = (x @ w_q.T).reshape(b, lq, H, DH)
        h_k = (key_value_states @ w_k.T).reshape(b, lk, H, DH)
        h_v = (key_value_states @ w_v.T).reshape(b, lk, H, DH)
        score = jnp.einsum('bqhd,bkhd->bhqk', h_q, h_k)
        score = score + position_bias[None]
        m = attention_mask[:, None]
        score = jnp.where(m, score, -jnp.inf)
        score = jax.nn.softmax(score, axis=-1)
        score = jnp.where(m, score, 0.0)
        attn = jnp.einsum('bhqk,bkhd->bqhd', score, h_v).reshape(b, lq, H * DH)
        out = attn @ w_out.T
        return hidden_states + out

    def _L0_ffn_ref(x, base_W, router_W, lora_A, lora_B):
        import jax, jax.numpy as jnp
        import numpy as np
        R = 16
        ALPHA = 32
        SCALING = ALPHA / R
        E = 8
        TOP_K = 2
        base = jnp.einsum('bsd,od->bso', x, base_W)
        logits = jnp.einsum('bsd,ed->bse', x, router_W)
        probs = jax.nn.softmax(logits.astype(jnp.float32), axis=-1)
        top_vals, top_idx = jax.lax.top_k(probs, TOP_K)
        rw = top_vals / jnp.sum(top_vals, axis=-1, keepdims=True)
        w_dense = jnp.sum(jax.nn.one_hot(top_idx, E, dtype=rw.dtype) * rw[..., None], axis=-2).astype(x.dtype)
        mid = jnp.einsum('bsd,edr->bser', x, lora_A)
        mid = mid * w_dense[..., None]
        inc = jnp.einsum('bser,erd->bsd', mid, lora_B)
        return base + inc * SCALING
    x = x + _L0_attn_ref(_layernorm(x, axis=-1), L0_attn_Wqkv, L0_attn_bqkv, L0_attn_Wo, L0_attn_bo)
    x = x + _L0_xattn_ref(_layernorm(x, axis=-1), ctx_4096, mask_BxSxS2_bk0, L0_xattn_position_bias, L0_xattn_ln_weight, L0_xattn_w_q, L0_xattn_w_k, L0_xattn_w_v, L0_xattn_w_out)
    x = x + _L0_ffn_ref(_layernorm(x, axis=-1), L0_ffn_base_W, L0_ffn_router_W, L0_ffn_lora_A, L0_ffn_lora_B)
    return x

_drawn_inputs = setup_inputs


def setup_inputs(seed=0):
    import zlib

    import numpy as np

    out = dict(_drawn_inputs(seed))
    spreads = {'L0_xattn_ln_weight': (1.0, 0.2)}
    factors = {'L0_attn_bqkv': 5.128, 'L0_attn_bo': 5.756}
    for name, (base, spread) in spreads.items():
        noise = np.random.default_rng([zlib.crc32(name.encode()), seed]).standard_normal(out[name].shape)
        drawn = base * np.exp(spread * noise) if base else spread * noise
        out[name] = jnp.asarray(drawn.astype(out[name].dtype))
    for name, factor in factors.items():
        out[name] = (out[name] * factor).astype(out[name].dtype)
    return out
```

```python
from contextlib import ExitStack

import concourse.bass as bass
from concourse import mybir

ALU = mybir.AluOpType
ACT = mybir.ActivationFunctionType
AX = mybir.AxisListType
F32 = mybir.dt.float32
F32R = mybir.dt.float32r

P = 128
B = 8
C = 512
KC = C // P
T = B * P
HEADS = 32
PAIR = 2
GROUPS = HEADS // PAIR
HALF = B // 2
BANK = 512
NE, NR = 8, 16
ROUTED = 256
PIECE = PAIR * C
QKA, WV, WO, QKB = range(4)
EPS = 1e-5
MASKED = -1e30
SCORE_SCALE = float(P) ** -0.5
LORA_SCALE = 32 / 16


def decoder_kernel(nc, x, ctx_t, mask, w_qkv, b_qkv, w_o, b_o, ln_w, pos_bias, weights, w_base, w_routed, w_lora_b, out):
    with ExitStack() as ctx:
        def sb(name, shape, dt=F32):
            return ctx.enter_context(nc.sbuf_tensor(name, shape, dt))

        def sem(name):
            return ctx.enter_context(nc.semaphore(name))

        acc = sb("acc", [P, B, C])
        rows = sb("rows", [P, B, C])
        xt = [sb("xt_hi", [P, KC, T], F32R), sb("xt_lo", [P, KC, T], F32R)]
        ct = [sb("ct_hi", [P, KC, T], F32R), sb("ct_lo", [P, KC, T], F32R)]
        raw = sb("raw", [P, 4, PIECE])
        w = [sb("w_hi", [P, 4, PIECE], F32R), sb("w_lo", [P, 4, PIECE], F32R)]
        raw_a = sb("raw_a", [P, KC * 3 * P + C])
        ot = [sb("ot_hi", [P, PAIR * T], F32R), sb("ot_lo", [P, PAIR * T], F32R)]
        qt = sb("qt", [P, T])
        kt = sb("kt", [P, T])
        v = sb("v", [P, B, PAIR * P])
        probs = sb("probs", [P, B, P])
        probs_t = sb("probs_t", [P, B, P])
        bias = sb("bias", [P, PAIR, P])
        bias_mask = sb("bias_mask", [P, B, P])
        mask_add = sb("mask_add", [P, B, P])
        mask_raw = sb("mask_raw", [P, B, P], mask.dtype)
        has_key = sb("has_key", [P, B])
        b_o_rows = probs_t[:, 0:C // P, :].rearrange("p b n -> p (b n)")
        b_qkv_cols = sb("b_qkv_cols", [P, 3])
        ln_w_cols = sb("ln_w_cols", [P, KC])
        ident = sb("ident", [P, P])
        earlier = sb("earlier", [P, NE, NE])
        minus_half = sb("minus_half", [P, HALF])
        stats = sb("stats", [P, B, 6])
        mean_var = sb("mean_var", [P, B, 2])
        shifted = sb("shifted", [P, B])
        rstd = sb("rstd", [P, B])
        rms = sb("rms", [P, B])
        neg_max = sb("neg_max", [P, B])
        sums = sb("sums", [P, B])
        inv = sb("inv", [P, B])
        row_scale = sb("row_scale", [P, B])
        logits = sb("logits", [P, B, NE])
        gates = sb("gates", [P, B, NE])
        beats, ties = (probs_t[:, n:n + 2, :].rearrange("p b (e j) -> p (b e) j", j=NE) for n in (0, 2))
        rank = sb("rank", [P, B, NE])
        top = sb("top", [P, B])
        top_sum = sb("top_sum", [P, B])

        w_qkv_s = [t[:, 0:KC * 3 * P].rearrange("p (c n) -> p c n", c=KC) for t in ot]
        w_o_s = [t[:, KC * 3 * P:KC * 3 * P + C] for t in ot]
        vt_a = v[:, :, :].rearrange("p b n -> p (b n)")[:, 0:T]
        vt_tiles = v[:, :, :].rearrange("p b n -> p (b n)")[:, T:2 * T]
        ffn_cols = KC * C + KC * ROUTED + C
        ffn_raw = rows[:, :, :].rearrange("p b n -> p (b n)")[:, 0:ffn_cols]
        ffn = [t[:, :, :].rearrange("p c n -> p (c n)") for t in ct]
        base_s = [t[:, 0:KC * C].rearrange("p (c n) -> p c n", c=KC) for t in ffn]
        routed_s = [t[:, KC * C:KC * (C + ROUTED)].rearrange("p (c n) -> p c n", c=KC) for t in ffn]
        lora_b_s = [t[:, KC * (C + ROUTED):ffn_cols] for t in ffn]

        bank = [ctx.enter_context(nc.psum_tensor(f"bank{i}", [P, BANK], F32)) for i in range(8)]
        QK, SC, TO, VO = bank[0:2], bank[2:4], bank[4:6], bank[6:8]
        ROWS_T = SC + TO

        x_loaded = [sem(f"x_loaded{b}") for b in range(B)]
        raw_loaded = [sem(f"raw_loaded{p}") for p in range(4)]
        raw_a_loaded = sem("raw_a_loaded")
        small_loaded = sem("small_loaded")
        mask_loaded = sem("mask_loaded")
        bias_loaded = sem("bias_loaded")
        ffn_loaded = sem("ffn_loaded")
        stored = sem("stored")
        ident_ready = sem("ident_ready")
        const_step = sem("const_step")
        consts_ready = sem("consts_ready")
        stats_step = sem("stats_step")
        stats_ready = sem("stats_ready")
        rstd_step = sem("rstd_step")
        rstd_ready = sem("rstd_ready")
        norm_step = sem("norm_step")
        rows_ready = sem("rows_ready")
        rows_t_done = sem("rows_t_done")
        xt_hi_ready = sem("xt_hi_ready")
        xt_lo_ready = sem("xt_lo_ready")
        ct_hi_ready = sem("ct_hi_ready")
        ct_lo_ready = sem("ct_lo_ready")
        wa_hi_ready = sem("wa_hi_ready")
        wa_lo_ready = sem("wa_lo_ready")
        w_hi_ready = [sem(f"w_hi_ready{p}") for p in range(4)]
        w_lo_ready = [sem(f"w_lo_ready{p}") for p in range(4)]
        ffn_hi_ready = sem("ffn_hi_ready")
        ffn_lo_ready = sem("ffn_lo_ready")
        qkv_done = sem("qkv_done")
        qkv_copied = sem("qkv_copied")
        values_turned = sem("values_turned")
        values_copied = sem("values_copied")
        bo_added = sem("bo_added")
        mask_step = sem("mask_step")
        mask_ready = sem("mask_ready")
        bias_mask_ready = sem("bias_mask_ready")
        qk_done = sem("qk_done")
        qk_copied = sem("qk_copied")
        v_done = sem("v_done")
        v_copied = sem("v_copied")
        scores_done = sem("scores_done")
        scores_biased = sem("scores_biased")
        max_ready = sem("max_ready")
        exp_done = sem("exp_done")
        inv_ready = sem("inv_ready")
        scale_ready = sem("scale_ready")
        probs_ready = sem("probs_ready")
        probs_turned = sem("probs_turned")
        probs_t0_copied = sem("probs_t0_copied")
        probs_t1_copied = sem("probs_t1_copied")
        pv_done = sem("pv_done")
        ot_hi_ready = sem("ot_hi_ready")
        ot_lo_ready = sem("ot_lo_ready")
        out_done = sem("out_done")
        out_added = sem("out_added")
        routed_done = sem("routed_done")
        route_step = sem("route_step")
        logits_ready = sem("logits_ready")
        gates_exp = sem("gates_exp")
        mid_ready = sem("mid_ready")
        mid_turned = sem("mid_turned")
        mid_hi_ready = sem("mid_hi_ready")
        mid_lo_ready = sem("mid_lo_ready")
        ffn_done = sem("ffn_done")
        result_ready = sem("result_ready")

        def half(i):
            return slice(HALF * i, HALF * (i + 1))

        def cols(i, n=P):
            return slice(n * i, n * (i + 1))

        def tiles(bank_ap):
            return bank_ap[:, :].rearrange("p (b n) -> p b n", b=HALF)

        block = ctx.enter_context(nc.Block())

        @block.sync
        def _(sp):
            for b in range(B):
                sp.dma_start(acc[:, b, :], x[:, b, :]).then_inc(x_loaded[b], 16)
            sp.dma_start(raw_a[:, 0:KC * 3 * P], w_qkv).then_inc(raw_a_loaded, 16)
            sp.dma_start(raw_a[:, KC * 3 * P:], w_o).then_inc(raw_a_loaded, 16)
            sp.dma_start(b_qkv_cols[:, :], b_qkv).then_inc(small_loaded, 16)
            sp.dma_start(ln_w_cols[:, :], ln_w).then_inc(small_loaded, 16)
            sp.dma_start(b_o_rows, b_o.partition_broadcast(P)).then_inc(small_loaded, 16)
            for c in range(KC):
                sp.dma_start(raw[:, c, :], ctx_t[:, c, :]).then_inc(raw_loaded[c], 16)
            sp.dma_start(mask_raw[:, :, :], mask).then_inc(mask_loaded, 16)
            sp.dma_start(bias[:, :, :], pos_bias[0]).then_inc(bias_loaded, 16)

            def load(piece, g):
                sp.dma_start(raw[:, piece, :], weights[g, piece]).then_inc(raw_loaded[piece], 16)

            for piece in range(4):
                sp.wait_ge(ct_lo_ready, piece + 1)
                load(piece, 0)
            for piece in (QKA, WV):
                sp.wait_ge(w_lo_ready[piece], 1)
                load(piece, 1)

            def refill(g, last=False):
                sp.wait_ge(w_lo_ready[QKB], g + 1)
                load(QKB, g + 1)
                sp.wait_ge(bias_mask_ready, PAIR * g + PAIR)
                sp.dma_start(bias[:, :, :], pos_bias[g + 1]).then_inc(bias_loaded, 16)
                if not last:
                    for piece in (QKA, WV):
                        sp.wait_ge(w_lo_ready[piece], g + 2)
                        load(piece, g + 2)
                sp.wait_ge(w_lo_ready[WO], g + 1)
                load(WO, g + 1)

            with sp.Fori(0, GROUPS - 2) as g:
                refill(g)
            refill(GROUPS - 2, last=True)
            n = 0
            for src, width in ((w_base, KC * C), (w_routed, KC * ROUTED), (w_lora_b, C)):
                sp.dma_start(ffn_raw[:, n:n + width], src).then_inc(ffn_loaded, 16)
                n += width
            for b in range(B):
                sp.wait_ge(result_ready, b + 1)
                sp.dma_start(out[:, b, :], acc[:, b, :]).then_inc(stored, 16)
            sp.wait_ge(stored, 16 * B)

        @block.gpsimd
        def _(pool):
            step = [0]

            def chained(ins):
                step[0] += 1
                ins.then_inc(const_step, 1)
                pool.wait_ge(const_step, step[0])

            chained(pool.memset(ident[:, :], 0.0))
            pool.affine_select(out=ident[:, :], in_=ident[:, :], compare_op=ALU.not_equal, fill=1.0, base=0,
                               pattern=[[-1, P]], channel_multiplier=1).then_inc(ident_ready, 1)
            chained(pool.memset(earlier[:, :, :], 1.0))
            pool.affine_select(out=earlier[:, :, :], in_=earlier[:, :, :], compare_op=ALU.is_gt, fill=0.0, base=0,
                               pattern=[[1, NE], [-1, NE]], channel_multiplier=0).then_inc(consts_ready, 1)
            chained(pool.memset(minus_half[:, :], -0.5))

            rstd_steps = [0]

            def rstd_chained(ins):
                rstd_steps[0] += 1
                ins.then_inc(rstd_step, 1)
                pool.wait_ge(rstd_step, rstd_steps[0])

            def root(layer, i):
                h = half(i)
                var = mean_var[:, h, 1]
                pool.wait_ge(stats_ready, 2 * layer + i + 1)
                rstd_chained(pool.tensor_scalar(shifted[:, h], var, 1.0, EPS, ALU.mult, ALU.add))
                ins = pool.tensor_tensor(rstd[:, h], shifted[:, h], minus_half[:, :], ALU.pow)
                if layer == 1:
                    rstd_chained(ins)
                    rstd_chained(pool.tensor_tensor(rms[:, h], rstd[:, h], rstd[:, h], ALU.mult))
                    rstd_chained(pool.tensor_tensor(rms[:, h], rms[:, h], var, ALU.mult))
                    rstd_chained(pool.tensor_scalar(rms[:, h], rms[:, h], 1.0, EPS, ALU.mult, ALU.add))
                    ins = pool.tensor_tensor(rms[:, h], rms[:, h], minus_half[:, :], ALU.pow)
                ins.then_inc(rstd_ready, 1)

            root(0, 0)
            root(0, 1)
            pool.wait_ge(wa_hi_ready, 1)
            pool.tensor_tensor(ot[1][:, :], raw_a[:, :], ot[0][:, :].bitcast(F32), ALU.subtract).then_inc(wa_lo_ready, 1)
            for c in range(KC):
                pool.wait_ge(ct_hi_ready, c + 1)
                pool.tensor_tensor(ct[1][:, c, :], raw[:, c, :], ct[0][:, c, :].bitcast(F32),
                                   ALU.subtract).then_inc(ct_lo_ready, 1)
            pool.wait_ge(mask_ready, 1)
            root(1, 0)
            root(1, 1)

            def add_mask(g):
                pool.wait_ge(bias_loaded, 16 * (g + 1))
                for j in range(PAIR):
                    pool.wait_ge(scores_biased, 2 * (PAIR * g + j + 1))
                    pool.tensor_tensor(bias_mask[:, :, :], mask_add[:, :, :],
                                       bias[:, j, :].unsqueeze(1).to_broadcast([P, B, P]),
                                       ALU.add).then_inc(bias_mask_ready, 1)

            with pool.Fori(0, GROUPS) as g:
                add_mask(g)
            root(2, 0)
            root(2, 1)

        @block.tensor
        def _(pe):
            def three_pass(out_ap, pairs, start=True, stop=True):
                n = len(pairs) * 3
                k = 0
                for lhs, rhs in pairs:
                    for a, b in ((0, 0), (0, 1), (1, 0)):
                        ins = pe.matmul(out_ap, lhs[a], rhs[b], start=start and k == 0, stop=stop and k == n - 1)
                        k += 1
                return ins

            def turn_rows(layer, i):
                pe.wait_ge(rows_ready, 2 * layer + i + 1)
                for c in range(KC):
                    n = KC * i + c
                    if n >= len(ROWS_T):
                        pe.wait_ge(xt_lo_ready, 2 * KC * layer + n - len(ROWS_T) + 1)
                    for t in range(HALF):
                        ins = pe.transpose(ROWS_T[n % len(ROWS_T)][:, cols(t)],
                                           rows[:, HALF * i + t, cols(c)], ident[:, :])
                    ins.then_inc(rows_t_done, 1)

            def scores(s, i):
                for t in range(HALF):
                    b = HALF * i + t
                    ins = pe.matmul(SC[i][:, cols(t)], qt[:, cols(b)], kt[:, cols(b)], start=True, stop=True)
                ins.then_inc(scores_done, 1)

            def turn_probs(s):
                for i in range(2):
                    pe.wait_ge(probs_ready, 2 * s + i + 1)
                    for t in range(HALF):
                        ins = pe.transpose(TO[i][:, cols(t)], probs[:, HALF * i + t, :], ident[:, :])
                    ins.then_inc(probs_turned, 1)

            def weigh_values(s, values):
                for i in range(2):
                    pe.wait_ge((probs_t0_copied, probs_t1_copied)[i], s + 1)
                    for t in range(HALF):
                        b = HALF * i + t
                        ins = pe.matmul(TO[i][:, cols(t)], values(b), probs_t[:, b, :], start=True, stop=True)
                    ins.then_inc(pv_done, 1)

            pe.wait_ge(ident_ready, 1)
            turn_rows(0, 0)
            turn_rows(0, 1)
            pe.wait_ge(wa_lo_ready, 1)
            for i in range(2):
                pe.wait_ge(xt_lo_ready, KC * (i + 1))
                for part in range(3):
                    n = 3 * i + part
                    if n >= 2:
                        pe.wait_ge(qkv_copied, n - 1)
                    three_pass(QK[n % 2][:, :],
                               [([s[:, c, cols(part)] for s in w_qkv_s], [s[:, c, cols(i, BANK)] for s in xt])
                                for c in range(KC)]).then_inc(qkv_done, 1)
            pe.wait_ge(qkv_copied, 6)
            for i in range(2):
                scores(0, i)
            for i in range(2):
                for t in range(HALF):
                    ins = pe.transpose(VO[i][:, cols(t)], vt_a[:, cols(HALF * i + t)], ident[:, :])
                ins.then_inc(values_turned, 1)
            turn_probs(0)
            pe.wait_ge(values_copied, 2)
            weigh_values(0, lambda b: vt_tiles[:, cols(b)])
            pe.wait_ge(ot_lo_ready, 2)
            for b in range(B):
                if b >= 2:
                    pe.wait_ge(out_added, b - 1)
                three_pass(VO[b % 2][:, :], [([s[:, cols(b)] for s in ot], w_o_s)]).then_inc(out_done, 1)
            turn_rows(1, 0)
            turn_rows(1, 1)

            def project_qk(g, j):
                piece = (QKA, QKB)[j]
                pe.wait_ge(w_lo_ready[piece], g + 1)
                for part, src in enumerate((xt, ct)):
                    for i in range(2):
                        n = 4 * (PAIR * g + j) + 2 * part + i
                        if j or part or not isinstance(g, int) or g:
                            pe.wait_ge(qk_copied, n - 1)
                        three_pass(QK[i][:, :],
                                   [([s[:, piece, cols(KC * part + c)] for s in w],
                                     [s[:, c, cols(i, BANK)] for s in src])
                                    for c in range(KC)]).then_inc(qk_done, 1)

            def project_v(g, first):
                pe.wait_ge(w_lo_ready[WV], g + 1)
                for b in range(B):
                    if b >= 2:
                        pe.wait_ge(v_copied, B * g + b - 1)
                    else:
                        pe.wait_ge(out_added, B if first else B * g)
                    three_pass(VO[b % 2][:, 0:PAIR * P],
                               [([s[:, c, cols(b)] for s in ct], [s[:, WV, cols(c, PAIR * P)] for s in w])
                                for c in range(KC)]).then_inc(v_done, 1)

            def project_out(g, v_before):
                pe.wait_ge(w_lo_ready[WO], g + 1)
                pe.wait_ge(ot_lo_ready, 2 + 2 * PAIR * (g + 1))
                for b in range(B):
                    if b >= 2:
                        pe.wait_ge(out_added, B * (g + 1) + b - 1)
                    else:
                        pe.wait_ge(v_copied, v_before)
                    three_pass(VO[b % 2][:, :],
                               [([s[:, cols(j * B + b)] for s in ot], [s[:, WO, cols(j, C)] for s in w])
                                for j in range(PAIR)]).then_inc(out_done, 1)

            def head_scores(h):
                pe.wait_ge(qk_copied, 4 * h + 4)
                for i in range(2):
                    pe.wait_ge(scores_biased, 2 * h + i + 1)
                    scores(h + 1, i)

            def turn_head_probs(h):
                pe.wait_ge(ot_lo_ready, 2 * (h + 1))
                turn_probs(h + 1)

            def weigh_head_values(g, j):
                pe.wait_ge(v_copied, B * (g + 1))
                weigh_values(PAIR * g + j + 1, lambda b: v[:, b, cols(j)])

            def group(g, first=False):
                project_qk(g, 0)
                if not first:
                    turn_head_probs(PAIR * g - 1)
                head_scores(PAIR * g)
                if not first:
                    weigh_head_values(g - 1, 1)
                project_v(g, first)
                turn_head_probs(PAIR * g)
                if not first:
                    project_out(g - 1, B * (g + 1))
                project_qk(g, 1)
                weigh_head_values(g, 0)
                head_scores(PAIR * g + 1)

            pe.wait_ge(xt_lo_ready, 4 * KC)
            pe.wait_ge(ct_lo_ready, KC)
            group(0, first=True)
            with pe.Fori(1, GROUPS) as g:
                group(g)
            turn_head_probs(HEADS - 1)
            weigh_head_values(GROUPS - 1, 1)
            project_out(GROUPS - 1, B * GROUPS)

            base_banks = QK + SC

            def routed(i):
                pe.wait_ge(xt_lo_ready, 2 * KC * 2 + KC * (i + 1))
                for t in range(HALF):
                    b = HALF * i + t
                    three_pass(VO[t // 2][:, cols(t % 2, ROUTED)],
                               [([s[:, c, cols(b)] for s in xt], [s[:, c, :] for s in routed_s])
                                for c in range(KC)]).then_inc(routed_done, 1)

            def base(i):
                for t in range(HALF):
                    b = HALF * i + t
                    if i:
                        pe.wait_ge(result_ready, t + 1)
                    elif t >= len(QK):
                        pe.wait_ge(xt_lo_ready, 2 * KC * 3)
                    three_pass(base_banks[t][:, :],
                               [([s[:, c, cols(b)] for s in xt], [s[:, c, :] for s in base_s])
                                for c in range(KC)], stop=False)

            def lora(i):
                pe.wait_ge(mid_ready, i + 1)
                for t in range(HALF):
                    ins = pe.transpose(TO[i][:, cols(t)], probs[:, HALF * i + t, :], ident[:, :])
                ins.then_inc(mid_turned, 1)
                pe.wait_ge(mid_lo_ready, i + 1)
                for t in range(HALF):
                    b = HALF * i + t
                    three_pass(base_banks[t][:, :], [([s[:, cols(b)] for s in ot], lora_b_s)],
                               start=False).then_inc(ffn_done, 1)

            turn_rows(2, 0)
            turn_rows(2, 1)
            pe.wait_ge(ffn_lo_ready, 1)
            pe.wait_ge(out_added, B * (GROUPS + 1))
            routed(0)
            base(0)
            pe.wait_ge(mid_ready, 1)
            routed(1)
            lora(0)
            base(1)
            lora(1)

        @block.scalar
        def _(act):
            def split_rows(layer, i):
                for c in range(KC):
                    n = KC * i + c
                    act.wait_ge(rows_t_done, 2 * KC * layer + n + 1)
                    to, of = xt[0][:, c, cols(i, BANK)], ROWS_T[n % len(ROWS_T)][:, :]
                    scale = ln_w_cols[:, c:c + 1] if layer == 1 else 1.0
                    act.activation(to, of, ACT.Copy, scale=scale).then_inc(xt_hi_ready, 1)

            def exponentials(s, i):
                act.wait_ge(max_ready, 2 * s + i + 1)
                for t in range(HALF):
                    b = HALF * i + t
                    ins = act.activation(probs[:, b, :], probs[:, b, :], ACT.Exp, bias=neg_max[:, b:b + 1],
                                         accum_out=sums[:, b:b + 1])
                ins.then_inc(exp_done, 1)

            def copy_probs_t(s):
                act.wait_ge(probs_turned, 2 * s + 1)
                act.copy(probs_t[:, half(0), :], tiles(TO[0])).then_inc(probs_t0_copied, 1)

            def split_out(s, j):
                for i in range(2):
                    act.wait_ge(pv_done, 2 * s + i + 1)
                    act.copy(ot[0][:, cols(2 * j + i, BANK)], TO[i][:, :]).then_inc(ot_hi_ready, 1)

            act.wait_ge(raw_a_loaded, 32)
            act.copy(ot[0][:, :], raw_a[:, :]).then_inc(wa_hi_ready, 1)
            split_rows(0, 0)
            split_rows(0, 1)
            act.wait_ge(small_loaded, 48)
            for i in range(2):
                for part in range(3):
                    act.wait_ge(qkv_done, 3 * i + part + 1)
                    act.activation((qt, kt, vt_a)[part][:, cols(i, BANK)], QK[(3 * i + part) % 2][:, :], ACT.Identity,
                                   bias=b_qkv_cols[:, part:part + 1]).then_inc(qkv_copied, 1)
            for c in range(KC):
                act.wait_ge(raw_loaded[c], 16)
                act.copy(ct[0][:, c, :], raw[:, c, :]).then_inc(ct_hi_ready, 1)
            exponentials(0, 0)
            exponentials(0, 1)
            copy_probs_t(0)
            split_out(0, 0)

            def split_weights(piece, g):
                act.wait_ge(raw_loaded[piece], 16 * (g + 2))
                act.copy(w[0][:, piece, :], raw[:, piece, :]).then_inc(w_hi_ready[piece], 1)

            split_weights(QKA, 0)
            split_weights(WV, 0)
            split_rows(1, 0)
            split_rows(1, 1)

            def copy_qk(g, j, k):
                n = 4 * (PAIR * g + j) + k
                act.wait_ge(qk_done, n + 1)
                act.copy((qt, kt)[k // 2][:, cols(k % 2, BANK)], QK[k % 2][:, :]).then_inc(qk_copied, 1)

            def copy_v(g, b):
                act.wait_ge(v_done, B * g + b + 1)
                act.copy(v[:, b, :], VO[b % 2][:, 0:PAIR * P]).then_inc(v_copied, 1)

            def group(g, first=False, last=False):
                if not first:
                    exponentials(PAIR * g, 0)
                copy_qk(g, 0, 0)
                if not first:
                    exponentials(PAIR * g, 1)
                copy_qk(g, 0, 1)
                if not first:
                    act.wait_ge(qk_done, 8 * g)
                split_weights(QKB, g)
                copy_qk(g, 0, 2)
                copy_qk(g, 0, 3)
                if not first:
                    copy_probs_t(PAIR * g)
                    split_out(PAIR * g, 1)
                copy_v(g, 0)
                exponentials(PAIR * g + 1, 0)
                copy_v(g, 1)
                copy_v(g, 2)
                exponentials(PAIR * g + 1, 1)
                for b in range(3, B):
                    copy_v(g, b)
                copy_probs_t(PAIR * g + 1)
                if not last:
                    act.wait_ge(qk_done, 8 * g + 4)
                    split_weights(QKA, g + 1)
                    act.wait_ge(v_done, B * (g + 1))
                    split_weights(WV, g + 1)
                act.wait_ge(out_done, B * (g + 1) if not first else B)
                split_weights(WO, g)
                for k in range(4):
                    copy_qk(g, 1, k)
                split_out(PAIR * g + 1, 0)

            group(0, first=True)
            with act.Fori(1, GROUPS - 1) as g:
                group(g)
            group(GROUPS - 1, last=True)
            exponentials(HEADS, 0)
            exponentials(HEADS, 1)
            act.wait_ge(ffn_loaded, 48)
            act.wait_ge(qk_done, 4 * HEADS)
            act.copy(ffn[0][:, 0:ffn_cols], ffn_raw[:, :]).then_inc(ffn_hi_ready, 1)
            copy_probs_t(HEADS)
            split_out(HEADS, 1)
            split_rows(2, 0)
            split_rows(2, 1)
            for i in range(2):
                act.wait_ge(logits_ready, i + 1)
                act.activation(gates[:, half(i), :], logits[:, half(i), :], ACT.Exp).then_inc(gates_exp, 1)
                act.wait_ge(mid_turned, i + 1)
                act.copy(ot[0][:, cols(i, BANK)], TO[i][:, :]).then_inc(mid_hi_ready, 1)

        @block.vector
        def _(dve):
            def row_stats(layer, i):
                for t in range(HALF):
                    b = HALF * i + t
                    if layer == 0:
                        dve.wait_ge(x_loaded[b], 16)
                    else:
                        dve.wait_ge(out_added, B * (1 if layer == 1 else GROUPS + 1) - B + b + 1)
                    dve.bn_stats(stats[:, b, :], acc[:, b, :]).then_inc(stats_step, 1)
                dve.wait_ge(stats_step, 2 * HALF * layer + HALF * (i + 1))
                for t in range(HALF):
                    b = HALF * i + t
                    ins = dve.bn_aggr(mean_var[:, b, :], stats[:, b, :])
                ins.then_inc(stats_ready, 1)

            norm_steps = [0]

            def normed(ins):
                norm_steps[0] += 1
                ins.then_inc(norm_step, 1)

            def normalise(layer, i):
                dve.wait_ge(rstd_ready, 2 * layer + i + 1)
                for t in range(HALF):
                    b = HALF * i + t
                    ins = dve.tensor_scalar(rows[:, b, :], acc[:, b, :], mean_var[:, b, 0:1], rstd[:, b:b + 1],
                                            ALU.subtract, ALU.mult)
                    if layer == 1:
                        normed(ins)
                if layer == 1:
                    for t in range(HALF):
                        b = HALF * i + t
                        dve.wait_ge(norm_step, norm_steps[0] - (HALF - 1 if t == 0 else HALF - 1))
                        normed(dve.tensor_tensor(acc[:, b, :], acc[:, b, :], rows[:, b, :], ALU.add))
                    dve.wait_ge(norm_step, norm_steps[0])
                    for t in range(HALF):
                        b = HALF * i + t
                        ins = dve.tensor_scalar(rows[:, b, :], rows[:, b, :], rms[:, b:b + 1], None, ALU.mult)
                ins.then_inc(rows_ready, 1)

            def split_rows(layer, i):
                for c in range(KC):
                    n = KC * i + c
                    dve.wait_ge(xt_hi_ready, 2 * KC * layer + n + 1)
                    of, hi = ROWS_T[n % len(ROWS_T)][:, :], xt[0][:, c, cols(i, BANK)].bitcast(F32)
                    to = xt[1][:, c, cols(i, BANK)]
                    if layer == 1:
                        ins = dve.scalar_tensor_tensor(out=to, in0=of, scalar=ln_w_cols[:, c:c + 1], in1=hi,
                                                       op0=ALU.mult, op1=ALU.subtract)
                    else:
                        ins = dve.tensor_tensor(to, of, hi, ALU.subtract)
                    ins.then_inc(xt_lo_ready, 1)

            def take_scores(s, i, add=True):
                dve.wait_ge(scores_done, 2 * s + i + 1)
                if add:
                    if i == 0:
                        dve.wait_ge(bias_mask_ready, s)
                    ins = dve.tensor_tensor(probs[:, half(i), :], tiles(SC[i]), bias_mask[:, half(i), :], ALU.add)
                else:
                    ins = dve.tensor_scalar(probs[:, half(i), :], tiles(SC[i]), SCORE_SCALE, None, ALU.mult)
                ins.then_inc(scores_biased, 1)

            def maxima(s, i):
                dve.wait_ge(scores_biased, 2 * s + i + 1)
                dve.tensor_reduce(neg_max[:, half(i)], probs[:, half(i), :], AX.X, ALU.max,
                                  negate=True).then_inc(max_ready, 1)

            def normalise_probs(s, i, masked=True):
                dve.wait_ge(exp_done, 2 * s + i + 1)
                dve.reciprocal(inv[:, half(i)], sums[:, half(i)]).then_inc(inv_ready, 1)
                dve.wait_ge(inv_ready, 2 * s + i + 1)
                scale = inv
                if masked:
                    dve.tensor_tensor(row_scale[:, half(i)], inv[:, half(i)], has_key[:, half(i)],
                                      ALU.mult).then_inc(scale_ready, 1)
                    dve.wait_ge(scale_ready, 2 * s - 2 + i + 1)
                    scale = row_scale
                dve.tensor_tensor(probs[:, half(i), :], probs[:, half(i), :],
                                  scale[:, half(i)].unsqueeze(2).to_broadcast([P, HALF, P]),
                                  ALU.mult).then_inc(probs_ready, 1)

            def copy_probs_t(s):
                dve.wait_ge(probs_turned, 2 * s + 2)
                dve.tensor_copy(probs_t[:, half(1), :], tiles(TO[1])).then_inc(probs_t1_copied, 1)

            def split_out(s, j):
                for i in range(2):
                    dve.wait_ge(ot_hi_ready, 2 * s + i + 1)
                    c = cols(2 * j + i, BANK)
                    dve.tensor_tensor(ot[1][:, c], TO[i][:, :], ot[0][:, c].bitcast(F32),
                                      ALU.subtract).then_inc(ot_lo_ready, 1)

            def add_out(n, b):
                dve.wait_ge(out_done, B * n + b + 1)
                dve.tensor_tensor(acc[:, b, :], VO[b % 2][:, :], acc[:, b, :], ALU.add).then_inc(out_added, 1)

            row_stats(0, 0)
            row_stats(0, 1)
            normalise(0, 0)
            normalise(0, 1)
            dve.wait_ge(small_loaded, 48)
            dve.wait_ge(rows_t_done, 1)
            for b in range(B):
                dve.tensor_tensor(acc[:, b, :], acc[:, b, :], b_o_rows, ALU.add).then_inc(bo_added, 1)
            split_rows(0, 0)
            split_rows(0, 1)
            dve.wait_ge(mask_loaded, 16)
            dve.tensor_scalar(mask_add[:, :, :], mask_raw[:, :, :], -1.0, -MASKED, ALU.add,
                              ALU.mult).then_inc(mask_ready, 1)
            dve.tensor_reduce(has_key[:, :], mask_raw[:, :, :], AX.X, ALU.max).then_inc(mask_step, 1)
            dve.wait_ge(mask_step, 1)
            for i in range(2):
                take_scores(0, i, add=False)
            for i in range(2):
                maxima(0, i)
            for i in range(2):
                dve.wait_ge(values_turned, i + 1)
                dve.tensor_copy(vt_tiles[:, cols(i, BANK)], VO[i][:, :]).then_inc(values_copied, 1)
            for i in range(2):
                normalise_probs(0, i, masked=False)
            copy_probs_t(0)
            split_out(0, 0)
            dve.wait_ge(bo_added, B)
            for b in range(B):
                add_out(0, b)

            def split_weights(piece, g):
                dve.wait_ge(w_hi_ready[piece], g + 1)
                dve.tensor_tensor(w[1][:, piece, :], raw[:, piece, :], w[0][:, piece, :].bitcast(F32),
                                  ALU.subtract).then_inc(w_lo_ready[piece], 1)

            row_stats(1, 0)
            row_stats(1, 1)
            split_weights(QKA, 0)
            split_weights(WV, 0)
            normalise(1, 0)
            normalise(1, 1)
            split_rows(1, 0)
            split_rows(1, 1)

            def group(g, first=False, last=False):
                if not first:
                    normalise_probs(PAIR * g, 0)
                    normalise_probs(PAIR * g, 1)
                split_weights(QKB, g)
                if not first:
                    copy_probs_t(PAIR * g)
                for i in range(2):
                    take_scores(PAIR * g + 1, i)
                for i in range(2):
                    maxima(PAIR * g + 1, i)
                if not first:
                    split_out(PAIR * g, 1)
                for i in range(2):
                    normalise_probs(PAIR * g + 1, i)
                copy_probs_t(PAIR * g + 1)
                if not first:
                    for b in range(B):
                        if b in (2, 5) and not last:
                            split_weights((QKA, WV)[b // 4], g + 1)
                        add_out(g, b)
                else:
                    split_weights(QKA, g + 1)
                    split_weights(WV, g + 1)
                split_weights(WO, g)
                split_out(PAIR * g + 1, 0)
                for i in range(2):
                    take_scores(PAIR * g + 2, i)
                for i in range(2):
                    maxima(PAIR * g + 2, i)

            group(0, first=True)
            with dve.Fori(1, GROUPS - 1) as g:
                group(g)
            group(GROUPS - 1, last=True)
            for i in range(2):
                normalise_probs(HEADS, i)
            dve.wait_ge(ffn_hi_ready, 1)
            dve.tensor_tensor(ffn[1][:, 0:ffn_cols], ffn_raw[:, :], ffn[0][:, 0:ffn_cols].bitcast(F32),
                              ALU.subtract).then_inc(ffn_lo_ready, 1)
            copy_probs_t(HEADS)
            split_out(HEADS, 1)
            for b in range(B):
                add_out(GROUPS, b)
            row_stats(2, 0)
            row_stats(2, 1)
            dve.wait_ge(ffn_lo_ready, 1)
            normalise(2, 0)
            normalise(2, 1)
            split_rows(2, 0)
            split_rows(2, 1)
            steps = [0]

            def chained(ins):
                steps[0] += 1
                ins.then_inc(route_step, 1)
                dve.wait_ge(route_step, steps[0])

            def route(i):
                h = half(i)
                dve.wait_ge(routed_done, HALF * (i + 1))
                for n in range(2):
                    tile_pair = VO[n][:, :].rearrange("p (t n) -> p t n", t=2)[:, :, NE * NR:NE * NR + NE]
                    ins = dve.tensor_copy(rank[:, HALF * i + 2 * n:HALF * i + 2 * n + 2, :], tile_pair)
                    chained(ins)
                chained(dve.tensor_reduce(top[:, h], rank[:, h, :], AX.X, ALU.max))
                dve.tensor_tensor(logits[:, h, :], rank[:, h, :], top[:, h].unsqueeze(2).to_broadcast([P, HALF, NE]),
                                  ALU.subtract).then_inc(logits_ready, 1)
                dve.wait_ge(gates_exp, i + 1)
                flat = gates[:, h, :].rearrange("p t e -> p (t e)")
                others = gates[:, h, :].unsqueeze(2).to_broadcast([P, HALF, NE, NE])
                own = flat.unsqueeze(2).to_broadcast([P, HALF * NE, NE]).rearrange("p (t e) j -> p t e j", e=NE)
                beats4 = beats[:, :, :].rearrange("p (t e) j -> p t e j", e=NE)
                ties4 = ties[:, :, :].rearrange("p (t e) j -> p t e j", e=NE)
                before = earlier[:, :, :].unsqueeze(1).to_broadcast([P, HALF, NE, NE])
                chained(dve.tensor_tensor(beats4, others, own, ALU.is_gt))
                chained(dve.tensor_tensor(ties4, others, own, ALU.is_equal))
                chained(dve.tensor_tensor(ties4, ties4, before, ALU.mult))
                chained(dve.tensor_tensor(beats[:, :, :], beats[:, :, :], ties[:, :, :], ALU.add))
                chained(dve.tensor_reduce(rank[:, h, :].rearrange("p t e -> p (t e)"), beats[:, :, :], AX.X, ALU.add))
                chained(dve.scalar_tensor_tensor(out=logits[:, h, :], in0=rank[:, h, :], scalar=1.5,
                                                 in1=gates[:, h, :], op0=ALU.is_lt, op1=ALU.mult))
                chained(dve.tensor_reduce(top_sum[:, h], logits[:, h, :], AX.X, ALU.add))
                chained(dve.reciprocal(top[:, h], top_sum[:, h]))
                chained(dve.scalar_tensor_tensor(out=rank[:, h, :], in0=logits[:, h, :], scalar=LORA_SCALE,
                                                 in1=top[:, h].unsqueeze(2).to_broadcast([P, HALF, NE]),
                                                 op0=ALU.mult, op1=ALU.mult))
                for t in range(HALF):
                    b = HALF * i + t
                    mids = VO[t // 2][:, ROUTED * (t % 2):ROUTED * (t % 2) + NE * NR].rearrange("p (e r) -> p e r", e=NE)
                    ins = dve.tensor_tensor(probs[:, b, :].rearrange("p (e r) -> p e r", e=NE), mids,
                                            rank[:, b, :].unsqueeze(2).to_broadcast([P, NE, NR]), ALU.mult)
                ins.then_inc(mid_ready, 1)

            def split_mid(i):
                dve.wait_ge(mid_hi_ready, i + 1)
                dve.tensor_tensor(ot[1][:, cols(i, BANK)], TO[i][:, :], ot[0][:, cols(i, BANK)].bitcast(F32),
                                  ALU.subtract).then_inc(mid_lo_ready, 1)

            def results(i):
                for t in range(HALF):
                    b = HALF * i + t
                    dve.wait_ge(ffn_done, b + 1)
                    dve.tensor_tensor(acc[:, b, :], (QK + SC)[t][:, :], acc[:, b, :], ALU.add).then_inc(result_ready, 1)

            dve.wait_ge(consts_ready, 1)
            route(0)
            split_mid(0)
            route(1)
            results(0)
            split_mid(1)
            results(1)


def kernel(x, ctx_4096, mask_BxSxS2_bk0, L0_attn_Wqkv, L0_attn_bqkv, L0_attn_Wo, L0_attn_bo,
           L0_xattn_position_bias, L0_xattn_ln_weight, L0_xattn_w_q, L0_xattn_w_k, L0_xattn_w_v, L0_xattn_w_out,
           L0_ffn_base_W, L0_ffn_router_W, L0_ffn_lora_A, L0_ffn_lora_B):
    import numpy as np
    import concourse.bacc as bacc
    from concourse.bass_utils import run_bass_kernel_spmd

    def chunked(a):
        a = np.asarray(a)
        return a.reshape(KC, P, a.shape[1]).transpose(1, 0, 2).reshape(P, KC * a.shape[1])

    f = np.float32
    q, k, v = (np.asarray(a).reshape(GROUPS, PAIR, P, KC, P) for a in (L0_xattn_w_q, L0_xattn_w_k, L0_xattn_w_v))
    pieces = np.empty((GROUPS, 4, P, PIECE), f)
    for j, piece in ((0, QKA), (1, QKB)):
        pieces[:, piece] = np.stack([a[:, j].transpose(0, 3, 2, 1) for a in (q, k)], axis=2).reshape(GROUPS, P, PIECE)
    pieces[:, WV] = v.transpose(0, 4, 3, 1, 2).reshape(GROUPS, P, PIECE)
    pieces[:, WO] = np.asarray(L0_xattn_w_out).T.reshape(GROUPS, PAIR, P, C).transpose(0, 2, 1, 3).reshape(
        GROUPS, P, PIECE)
    routed = np.zeros((C, ROUTED), f)
    routed[:, 0:NE * NR] = np.asarray(L0_ffn_lora_A).transpose(1, 0, 2).reshape(C, NE * NR)
    routed[:, NE * NR:NE * NR + NE] = np.asarray(L0_ffn_router_W).T
    arrays = {
        "x": np.asarray(x).transpose(1, 0, 2),
        "ctx_t": np.asarray(ctx_4096).reshape(T, KC, P).transpose(2, 1, 0),
        "mask": np.asarray(mask_BxSxS2_bk0).transpose(1, 0, 2),
        "w_qkv": chunked(L0_attn_Wqkv),
        "b_qkv": np.asarray(L0_attn_bqkv).reshape(3, P).T,
        "w_o": np.asarray(L0_attn_Wo),
        "b_o": np.asarray(L0_attn_bo),
        "ln_w": np.asarray(L0_xattn_ln_weight).reshape(KC, P).T,
        "pos_bias": np.asarray(L0_xattn_position_bias).reshape(GROUPS, PAIR, P, P).transpose(0, 2, 1, 3),
        "weights": pieces,
        "w_base": chunked(np.asarray(L0_ffn_base_W).T),
        "w_routed": chunked(routed),
        "w_lora_b": np.asarray(L0_ffn_lora_B).reshape(NE * NR, C),
    }
    nc = bacc.Bacc("TRN2", target_bir_lowering=False, num_devices=1)
    sent, args = {}, []
    for name, a in arrays.items():
        a = np.ascontiguousarray(a)
        sent[f"in_{name}"] = a
        args.append(nc.dram_tensor(f"in_{name}", a.shape, mybir.dt.from_np(a.dtype), kind="ExternalInput").ap())
    args.append(nc.dram_tensor("out_rows", (P, B, C), F32, kind="ExternalOutput").ap())
    decoder_kernel(nc, *args)
    result = run_bass_kernel_spmd(nc, [sent], core_ids=[0])
    return np.ascontiguousarray(result.results[0]["out_rows"].transpose(1, 0, 2))
```

```python
from contextlib import ExitStack

import concourse.bass as bass
from concourse import mybir

ALU = mybir.AluOpType
ACT = mybir.ActivationFunctionType
AX = mybir.AxisListType
F32 = mybir.dt.float32
F32R = mybir.dt.float32r

P = 128
B = 8
C = 512
KC = C // P
T = B * P
HEADS = 32
PAIR = 2
GROUPS = HEADS // PAIR
HALF = B // 2
BANK = 512
NE, NR = 8, 16
ROUTED = 256
QKV_COLS, OUT_COLS = slice(0, KC * 3 * P), slice(KC * 3 * P, KC * 3 * P + C)
PIECE = PAIR * C
QKA, WV, WO, QKB = range(4)
EPS = 1e-5
MASKED = -1e30
SCORE_SCALE = float(P) ** -0.5
LORA_SCALE = 32 / 16


def decoder_kernel(nc, x, ctx_t, mask, w_qkv, b_qkv, w_o, b_o, ln_w, pos_bias, weights, w_base, w_routed, w_lora_b, out):
    with ExitStack() as ctx:
        def sb(name, shape, dt=F32):
            return ctx.enter_context(nc.sbuf_tensor(name, shape, dt))

        def sem(name):
            return ctx.enter_context(nc.semaphore(name))

        acc = sb("acc", [P, B, C])
        rows = sb("rows", [P, B, C])
        xt = [sb("xt_hi", [P, KC, T], F32R), sb("xt_lo", [P, KC, T], F32R)]
        ct = [sb("ct_hi", [P, KC, T], F32R), sb("ct_lo", [P, KC, T], F32R)]
        raw = sb("raw", [P, 4, PIECE])
        w = [sb("w_hi", [P, 4, PIECE], F32R), sb("w_lo", [P, 4, PIECE], F32R)]
        raw_a = sb("raw_a", [P, KC * 3 * P + C])
        ot = [sb("ot_hi", [P, PAIR * T], F32R), sb("ot_lo", [P, PAIR * T], F32R)]
        qt = sb("qt", [P, T])
        kt = sb("kt", [P, T])
        v = sb("v", [P, B, PAIR * P])
        probs = sb("probs", [P, B, P])
        probs_t = sb("probs_t", [P, B, P])
        bias = sb("bias", [P, PAIR, P])
        bias_mask = sb("bias_mask", [P, B, P])
        mask_add = sb("mask_add", [P, B, P])
        mask_raw = sb("mask_raw", [P, B, P], mask.dtype)
        has_key = sb("has_key", [P, B])
        b_o_rows = bias_mask[:, 0:C // P, :].rearrange("p b n -> p (b n)")
        b_qkv_cols = sb("b_qkv_cols", [P, 3])
        ln_w_cols = sb("ln_w_cols", [P, KC])
        ident = sb("ident", [P, P])
        earlier = sb("earlier", [P, NE, NE])
        minus_half = sb("minus_half", [P, 2, HALF])
        stats = sb("stats", [P, B, 6])
        mean_var = sb("mean_var", [P, B, 2])
        spread = sb("spread", [P, 2, B])
        rstd = sb("rstd", [P, 2, B])
        rstd_rms = sb("rstd_rms", [P, B])
        neg_mean = sb("neg_mean", [P, B])
        gain = sb("gain", [P, B])
        offset = sb("offset", [P, B])
        shift = sb("shift", [P, B])
        neg_max = sb("neg_max", [P, B])
        sums = sb("sums", [P, B])
        inv = sb("inv", [P, B])
        row_scale = sb("row_scale", [P, B])
        logits = sb("logits", [P, B, NE])
        gates = sb("gates", [P, B, NE])
        beats, ties = (probs_t[:, n:n + 2, :].rearrange("p b (e j) -> p (b e) j", j=NE) for n in (0, 2))
        rank = sb("rank", [P, B, NE])
        top = sb("top", [P, B])
        top_sum = sb("top_sum", [P, B])

        w_qkv_s = [t[:, QKV_COLS].rearrange("p (c n) -> p c n", c=KC) for t in ot]
        w_o_s = [t[:, OUT_COLS] for t in ot]
        vt_a = v[:, :, :].rearrange("p b n -> p (b n)")[:, 0:T]
        vt_tiles = v[:, :, :].rearrange("p b n -> p (b n)")[:, T:2 * T]
        ffn_cols = KC * C + KC * ROUTED + C
        ffn_raw = rows[:, :, :].rearrange("p b n -> p (b n)")[:, 0:ffn_cols]
        ffn = [t[:, :, :].rearrange("p c n -> p (c n)") for t in ct]
        base_s = [t[:, 0:KC * C].rearrange("p (c n) -> p c n", c=KC) for t in ffn]
        routed_s = [t[:, KC * C:KC * (C + ROUTED)].rearrange("p (c n) -> p c n", c=KC) for t in ffn]
        lora_b_s = [t[:, KC * (C + ROUTED):ffn_cols] for t in ffn]

        bank = [ctx.enter_context(nc.psum_tensor(f"bank{i}", [P, BANK], F32)) for i in range(8)]
        QK, SC, TO, VO = bank[0:2], bank[2:4], bank[4:6], bank[6:8]
        ROWS_T = SC + TO
        OWN_OUT = (SC + QK) * 2
        LAST_OUT = (SC + VO + QK) + SC

        x_loaded = [sem(f"x_loaded{b}") for b in range(B)]
        raw_loaded = [sem(f"raw_loaded{p}") for p in range(4)]
        raw_qkv_loaded = sem("raw_qkv_loaded")
        raw_o_loaded = sem("raw_o_loaded")
        small_loaded = sem("small_loaded")
        mask_loaded = sem("mask_loaded")
        bias_loaded = sem("bias_loaded")
        ffn_loaded = sem("ffn_loaded")
        stored = sem("stored")
        ident_ready = sem("ident_ready")
        const_step = sem("const_step")
        consts_ready = sem("consts_ready")
        stats_step = sem("stats_step")
        spread_step = sem("spread_step")
        spread_ready = sem("spread_ready")
        rstd_step = sem("rstd_step")
        rstd_ready = sem("rstd_ready")
        norm_step = sem("norm_step")
        residual_added = sem("residual_added")
        rows_ready = sem("rows_ready")
        rows_t_done = sem("rows_t_done")
        xt_hi_ready = sem("xt_hi_ready")
        xt_lo_ready = sem("xt_lo_ready")
        ct_hi_ready = sem("ct_hi_ready")
        ct_lo_ready = sem("ct_lo_ready")
        w_qkv_hi_ready = sem("w_qkv_hi_ready")
        w_qkv_lo_ready = sem("w_qkv_lo_ready")
        w_o_hi_ready = sem("w_o_hi_ready")
        w_o_lo_ready = sem("w_o_lo_ready")
        w_hi_ready = [sem(f"w_hi_ready{p}") for p in range(4)]
        w_lo_ready = [sem(f"w_lo_ready{p}") for p in range(4)]
        ffn_hi_ready = sem("ffn_hi_ready")
        ffn_lo_ready = sem("ffn_lo_ready")
        qkv_done = sem("qkv_done")
        qkv_copied = sem("qkv_copied")
        values_turned = sem("values_turned")
        values_copied = sem("values_copied")
        bo_added = sem("bo_added")
        mask_step = sem("mask_step")
        mask_ready = sem("mask_ready")
        bias_mask_ready = sem("bias_mask_ready")
        qk_done = sem("qk_done")
        qk_copied = sem("qk_copied")
        v_done = sem("v_done")
        v_copied = sem("v_copied")
        scores_done = sem("scores_done")
        scores_biased = sem("scores_biased")
        max_ready = sem("max_ready")
        exp_done = sem("exp_done")
        inv_ready = sem("inv_ready")
        scale_ready = sem("scale_ready")
        probs_ready = sem("probs_ready")
        probs_turned = sem("probs_turned")
        probs_t0_copied = sem("probs_t0_copied")
        probs_t1_copied = sem("probs_t1_copied")
        pv_done = sem("pv_done")
        ot_hi_ready = sem("ot_hi_ready")
        ot_lo_ready = sem("ot_lo_ready")
        out_done = sem("out_done")
        out_added = sem("out_added")
        routed_done = sem("routed_done")
        route_step = sem("route_step")
        logits_ready = sem("logits_ready")
        gates_exp = sem("gates_exp")
        mid_ready = sem("mid_ready")
        mid_turned = sem("mid_turned")
        mid_hi_ready = sem("mid_hi_ready")
        mid_lo_ready = sem("mid_lo_ready")
        ffn_done = sem("ffn_done")
        result_ready = sem("result_ready")

        def half(i):
            return slice(HALF * i, HALF * (i + 1))

        def cols(i, n=P):
            return slice(n * i, n * (i + 1))

        def tiles(bank_ap):
            return bank_ap[:, :].rearrange("p (b n) -> p b n", b=HALF)

        block = ctx.enter_context(nc.Block())

        @block.sync
        def _(sp):
            for b in range(HALF):
                sp.dma_start(acc[:, b, :], x[:, b, :]).then_inc(x_loaded[b], 16)
            sp.dma_start(raw_a[:, QKV_COLS], w_qkv).then_inc(raw_qkv_loaded, 16)
            for b in range(HALF, B):
                sp.dma_start(acc[:, b, :], x[:, b, :]).then_inc(x_loaded[b], 16)
            sp.dma_start(raw_a[:, OUT_COLS], w_o).then_inc(raw_o_loaded, 16)
            sp.dma_start(b_qkv_cols[:, :], b_qkv).then_inc(small_loaded, 16)
            sp.dma_start(ln_w_cols[:, :], ln_w).then_inc(small_loaded, 16)
            sp.dma_start(b_o_rows, b_o.partition_broadcast(P)).then_inc(small_loaded, 16)
            for c in range(KC):
                sp.dma_start(raw[:, c, :], ctx_t[:, c, :]).then_inc(raw_loaded[c], 16)
            sp.dma_start(mask_raw[:, :, :], mask).then_inc(mask_loaded, 16)
            sp.dma_start(bias[:, :, :], pos_bias[0]).then_inc(bias_loaded, 16)

            def load(piece, g):
                sp.dma_start(raw[:, piece, :], weights[g, piece]).then_inc(raw_loaded[piece], 16)

            for piece in range(4):
                sp.wait_ge(ct_lo_ready, piece + 1)
                load(piece, 0)
            for piece in (QKA, WV):
                sp.wait_ge(w_lo_ready[piece], 1)
                load(piece, 1)

            def refill(g, last=False):
                sp.wait_ge(w_lo_ready[QKB], g + 1)
                load(QKB, g + 1)
                sp.wait_ge(bias_mask_ready, PAIR * g + PAIR)
                sp.dma_start(bias[:, :, :], pos_bias[g + 1]).then_inc(bias_loaded, 16)
                if not last:
                    for piece in (QKA, WV):
                        sp.wait_ge(w_lo_ready[piece], g + 2)
                        load(piece, g + 2)
                sp.wait_ge(w_lo_ready[WO], g + 1)
                load(WO, g + 1)

            with sp.Fori(0, GROUPS - 2) as g:
                refill(g)
            refill(GROUPS - 2, last=True)
            n = 0
            for src, width in ((w_base, KC * C), (w_routed, KC * ROUTED), (w_lora_b, C)):
                sp.dma_start(ffn_raw[:, n:n + width], src).then_inc(ffn_loaded, 16)
                n += width
            for b in range(B):
                sp.wait_ge(result_ready, b + 1)
                sp.dma_start(out[:, b, :], acc[:, b, :]).then_inc(stored, 16)
            sp.wait_ge(stored, 16 * B)

        @block.gpsimd
        def _(pool):
            step = [0]

            def chained(ins):
                step[0] += 1
                ins.then_inc(const_step, 1)
                pool.wait_ge(const_step, step[0])

            chained(pool.memset(ident[:, :], 0.0))
            pool.affine_select(out=ident[:, :], in_=ident[:, :], compare_op=ALU.not_equal, fill=1.0, base=0,
                               pattern=[[-1, P]], channel_multiplier=1).then_inc(ident_ready, 1)
            chained(pool.memset(earlier[:, :, :], 1.0))
            pool.affine_select(out=earlier[:, :, :], in_=earlier[:, :, :], compare_op=ALU.is_gt, fill=0.0, base=0,
                               pattern=[[1, NE], [-1, NE]], channel_multiplier=0).then_inc(consts_ready, 1)
            chained(pool.memset(minus_half[:, :, :], -0.5))

            rstd_steps = [0]

            def rstd_chained(ins):
                rstd_steps[0] += 1
                ins.then_inc(rstd_step, 1)
                pool.wait_ge(rstd_step, rstd_steps[0])

            def root(layer, i):
                h, n = half(i), 2 if layer == 1 else 1
                pool.wait_ge(spread_ready, 2 * layer + i + 1)
                ins = pool.tensor_tensor(rstd[:, 0:n, h], spread[:, 0:n, h], minus_half[:, 0:n, :], ALU.pow)
                if layer == 1:
                    rstd_chained(ins)
                    ins = pool.tensor_tensor(rstd_rms[:, h], rstd[:, 0, h], rstd[:, 1, h], ALU.mult)
                if layer:
                    scale = rstd_rms if layer == 1 else rstd[:, 0, :]
                    rstd_chained(ins)
                    ins = pool.tensor_tensor(shift[:, h], neg_mean[:, h], scale[:, h], ALU.mult)
                ins.then_inc(rstd_ready, 1)

            root(0, 0)
            root(0, 1)
            pool.wait_ge(w_o_hi_ready, 1)
            pool.tensor_tensor(ot[1][:, OUT_COLS], raw_a[:, OUT_COLS], ot[0][:, OUT_COLS].bitcast(F32),
                               ALU.subtract).then_inc(w_o_lo_ready, 1)
            for c in range(KC):
                pool.wait_ge(ct_hi_ready, c + 1)
                pool.tensor_tensor(ct[1][:, c, :], raw[:, c, :], ct[0][:, c, :].bitcast(F32),
                                   ALU.subtract).then_inc(ct_lo_ready, 1)
            root(1, 0)
            root(1, 1)
            pool.wait_ge(mask_ready, 1)

            def add_mask(g):
                pool.wait_ge(bias_loaded, 16 * (g + 1))
                for j in range(PAIR):
                    pool.wait_ge(scores_biased, 2 * (PAIR * g + j + 1))
                    pool.tensor_tensor(bias_mask[:, :, :], mask_add[:, :, :],
                                       bias[:, j, :].unsqueeze(1).to_broadcast([P, B, P]),
                                       ALU.add).then_inc(bias_mask_ready, 1)

            with pool.Fori(0, GROUPS) as g:
                add_mask(g)
            pool.wait_ge(ffn_hi_ready, 1)
            pool.tensor_tensor(ffn[1][:, 0:ffn_cols], ffn_raw[:, :], ffn[0][:, 0:ffn_cols].bitcast(F32),
                               ALU.subtract).then_inc(ffn_lo_ready, 1)
            root(2, 0)
            root(2, 1)

        @block.tensor
        def _(pe):
            def three_pass(out_ap, pairs, start=True, stop=True):
                n = len(pairs) * 3
                k = 0
                for lhs, rhs in pairs:
                    for a, b in ((0, 0), (0, 1), (1, 0)):
                        ins = pe.matmul(out_ap, lhs[a], rhs[b], start=start and k == 0, stop=stop and k == n - 1)
                        k += 1
                return ins

            def turn_rows(layer, i):
                if i == 0 and layer:
                    pe.wait_ge(out_added, (0, B, B * (GROUPS + 1))[layer])
                pe.wait_ge(rows_ready, 2 * layer + i + 1)
                for c in range(KC):
                    n = KC * i + c
                    if n >= len(ROWS_T):
                        pe.wait_ge(xt_lo_ready, 2 * KC * layer + n - len(ROWS_T) + 1)
                    for t in range(HALF):
                        ins = pe.transpose(ROWS_T[n % len(ROWS_T)][:, cols(t)],
                                           rows[:, HALF * i + t, cols(c)], ident[:, :])
                    ins.then_inc(rows_t_done, 1)

            def scores(s, i):
                for t in range(HALF):
                    b = HALF * i + t
                    ins = pe.matmul(SC[i][:, cols(t)], qt[:, cols(b)], kt[:, cols(b)], start=True, stop=True)
                ins.then_inc(scores_done, 1)

            def turn_probs(s, halves=(0, 1), banks=TO):
                for i in halves:
                    pe.wait_ge(probs_ready, 2 * s + i + 1)
                    for t in range(HALF):
                        ins = pe.transpose(banks[i][:, cols(t)], probs[:, HALF * i + t, :], ident[:, :])
                    ins.then_inc(probs_turned, 1)

            def weigh_values(s, values, halves=(0, 1)):
                for i in halves:
                    pe.wait_ge((probs_t0_copied, probs_t1_copied)[i], s + 1)
                    for t in range(HALF):
                        b = HALF * i + t
                        ins = pe.matmul(TO[i][:, cols(t)], values(b), probs_t[:, b, :], start=True, stop=True)
                    ins.then_inc(pv_done, 1)

            def project_qk(g, j, steps=range(4), done=0):
                piece = (QKA, QKB)[j]
                pe.wait_ge(w_lo_ready[piece], g + 1)
                for k in steps:
                    part, i = k // 2, k % 2
                    if done >= 2 or j or not isinstance(g, int) or g:
                        pe.wait_ge(qk_copied, 4 * (PAIR * g + j) + done - 1)
                    three_pass(QK[i][:, :],
                               [([s[:, piece, cols(KC * part + c)] for s in w],
                                 [s[:, c, cols(i, BANK)] for s in (xt, ct)[part]])
                                for c in range(KC)]).then_inc(qk_done, 1)
                    done += 1

            def project_v(g, some=range(B), first=False):
                pe.wait_ge(w_lo_ready[WV], g + 1)
                for b in some:
                    if b >= 2:
                        pe.wait_ge(v_copied, B * g + b - 1)
                    elif first:
                        pe.wait_ge(values_copied, b + 1)
                    else:
                        pe.wait_ge(out_added, B * g)
                    three_pass(VO[b % 2][:, 0:PAIR * P],
                               [([s[:, c, cols(b)] for s in ct], [s[:, WV, cols(c, PAIR * P)] for s in w])
                                for c in range(KC)]).then_inc(v_done, 1)

            def project_out(g, v_before):
                pe.wait_ge(w_lo_ready[WO], g + 1)
                pe.wait_ge(ot_lo_ready, 2 + 2 * PAIR * (g + 1))
                for b in range(B):
                    if b >= 2:
                        pe.wait_ge(out_added, B * (g + 1) + b - 1)
                    else:
                        pe.wait_ge(v_copied, v_before)
                    three_pass(VO[b % 2][:, :],
                               [([s[:, cols(j * B + b)] for s in ot], [s[:, WO, cols(j, C)] for s in w])
                                for j in range(PAIR)]).then_inc(out_done, 1)

            def head_scores(h):
                pe.wait_ge(qk_copied, 4 * h + 4)
                for i in range(2):
                    pe.wait_ge(scores_biased, 2 * h + i + 1)
                    scores(h + 1, i)

            def turn_head_probs(h):
                pe.wait_ge(ot_lo_ready, 2 * (h + 1))
                turn_probs(h + 1)

            def weigh_head_values(g, j):
                pe.wait_ge(v_copied, B * (g + 1))
                weigh_values(PAIR * g + j + 1, lambda b: v[:, b, cols(j)])

            def group(g, last=False):
                project_qk(g, 0)
                turn_head_probs(PAIR * g - 1)
                head_scores(PAIR * g)
                weigh_head_values(g - 1, 1)
                project_v(g)
                turn_head_probs(PAIR * g)
                if last:
                    project_qk(g, 1)
                    head_scores(PAIR * g + 1)
                    weigh_head_values(g, 0)
                    project_out(g - 1, B * (g + 1))
                else:
                    project_out(g - 1, B * (g + 1))
                    project_qk(g, 1)
                    weigh_head_values(g, 0)
                    head_scores(PAIR * g + 1)

            def last_out():
                g = GROUPS - 1

                def part(b, j):
                    return three_pass(LAST_OUT[b][:, :],
                                      [([s[:, cols(j * B + b)] for s in ot], [s[:, WO, cols(j, C)] for s in w])],
                                      start=(j == 0), stop=(j == 1))

                pe.wait_ge(qk_copied, 4 * HEADS)
                turn_probs(HEADS, banks=QK)
                pe.wait_ge(w_lo_ready[WO], GROUPS)
                pe.wait_ge(ot_lo_ready, 2 * HEADS)
                pe.wait_ge(scores_biased, 2 * HEADS + 2)
                part(0, 0)
                part(1, 0)
                pe.wait_ge(out_added, B * GROUPS)
                part(2, 0)
                part(3, 0)
                weigh_head_values(g, 1)
                part(4, 0)
                part(5, 0)
                pe.wait_ge(ot_lo_ready, 2 * HEADS + 2)
                for b in range(B):
                    if b >= 6:
                        pe.wait_ge(out_added, B * GROUPS + b - 6 + 1)
                        part(b, 0)
                    part(b, 1).then_inc(out_done, 1)

            def follow_rows(out_ap, lhs, layer, i):
                for c in range(KC):
                    pe.wait_ge(xt_lo_ready, 2 * KC * layer + KC * i + c + 1)
                    ins = three_pass(out_ap, [(lhs(c), [s[:, c, cols(i, BANK)] for s in xt])],
                                     start=(c == 0), stop=(c == KC - 1))
                return ins

            def project_qkv(i, parts=(0, 1, 2)):
                for part in parts:
                    n = 3 * i + part
                    if n >= 2:
                        pe.wait_ge(qkv_copied, n - 1)
                    follow_rows(QK[n % 2][:, :], lambda c: [s[:, c, cols(part)] for s in w_qkv_s],
                                0, i).then_inc(qkv_done, 1)

            def turn_values(i):
                pe.wait_ge(qkv_copied, 3 * (i + 1))
                for t in range(HALF):
                    ins = pe.transpose(VO[i][:, cols(t)], vt_a[:, cols(HALF * i + t)], ident[:, :])
                ins.then_inc(values_turned, 1)

            def own_values(i):
                pe.wait_ge(values_copied, i + 1)
                weigh_values(0, lambda b: vt_tiles[:, cols(b)], (i,))

            def own_out(i):
                pe.wait_ge(ot_lo_ready, i + 1)
                pe.wait_ge(w_o_lo_ready, 1)
                for b in range(HALF * i, HALF * (i + 1)):
                    if i:
                        pe.wait_ge(out_added, b - HALF + 1)
                    elif b >= len(SC):
                        pe.wait_ge(qk_copied, b - len(SC) + 1)
                    three_pass(OWN_OUT[b][:, :], [([s[:, cols(b)] for s in ot], w_o_s)]).then_inc(out_done, 1)

            pe.wait_ge(ident_ready, 1)
            turn_rows(0, 0)
            pe.wait_ge(w_qkv_lo_ready, 1)
            project_qkv(0)
            turn_rows(0, 1)
            turn_values(0)
            project_qkv(1, (0,))
            pe.wait_ge(xt_lo_ready, 2 * KC)
            scores(0, 0)
            project_qkv(1, (1, 2))
            pe.wait_ge(qkv_copied, 5)
            scores(0, 1)
            turn_values(1)
            turn_probs(0, (0,))
            pe.wait_ge(ct_lo_ready, KC)
            pe.wait_ge(qkv_copied, 6)
            project_qk(0, 0, (2,), 0)
            own_values(0)
            project_qk(0, 0, (3,), 1)
            turn_probs(0, (1,))
            own_out(0)
            project_v(0, (0,), first=True)
            own_values(1)
            project_v(0, (1,), first=True)
            own_out(1)
            project_v(0, range(2, B))
            for i in range(2):
                turn_rows(1, i)
                pe.wait_ge(qk_copied, i + 1)
                follow_rows(QK[i][:, :], lambda c: [s[:, QKA, cols(c)] for s in w], 1, i).then_inc(qk_done, 1)
            project_qk(0, 1, (0,), 0)
            head_scores(0)
            project_qk(0, 1, (1, 2, 3), 1)
            turn_head_probs(0)
            weigh_head_values(0, 0)
            head_scores(1)
            with pe.Fori(1, GROUPS - 1) as g:
                group(g)
            group(GROUPS - 1, last=True)
            last_out()

            base_banks = QK + SC

            def routed(i):
                pe.wait_ge(xt_lo_ready, 2 * KC * 2 + KC * (i + 1))
                for t in range(HALF):
                    b = HALF * i + t
                    three_pass(VO[t // 2][:, cols(t % 2, ROUTED)],
                               [([s[:, c, cols(b)] for s in xt], [s[:, c, :] for s in routed_s])
                                for c in range(KC)]).then_inc(routed_done, 1)

            def base(i, some):
                for t in some:
                    b = HALF * i + t
                    if i:
                        pe.wait_ge(result_ready, t + 1)
                    elif t >= len(QK):
                        pe.wait_ge(xt_lo_ready, 2 * KC * 3)
                    three_pass(base_banks[t][:, :],
                               [([s[:, c, cols(b)] for s in xt], [s[:, c, :] for s in base_s])
                                for c in range(KC)], stop=False)

            def turn_mids(i):
                pe.wait_ge(mid_ready, i + 1)
                for t in range(HALF):
                    ins = pe.transpose(TO[i][:, cols(t)], probs[:, HALF * i + t, :], ident[:, :])
                ins.then_inc(mid_turned, 1)

            def lora(i):
                pe.wait_ge(mid_lo_ready, i + 1)
                for t in range(HALF):
                    b = HALF * i + t
                    three_pass(base_banks[t][:, :], [([s[:, cols(b)] for s in ot], lora_b_s)],
                               start=False).then_inc(ffn_done, 1)

            turn_rows(2, 0)
            pe.wait_ge(ffn_lo_ready, 1)
            routed(0)
            base(0, (0, 1))
            turn_rows(2, 1)
            base(0, (2, 3))
            turn_mids(0)
            routed(1)
            lora(0)
            base(1, (0, 1, 2))
            turn_mids(1)
            base(1, (3,))
            lora(1)

        @block.scalar
        def _(act):
            def split_rows(layer, i):
                for c in range(KC):
                    n = KC * i + c
                    act.wait_ge(rows_t_done, 2 * KC * layer + n + 1)
                    to, of = xt[0][:, c, cols(i, BANK)], ROWS_T[n % len(ROWS_T)][:, :]
                    scale = ln_w_cols[:, c:c + 1] if layer == 1 else 1.0
                    act.activation(to, of, ACT.Copy, scale=scale).then_inc(xt_hi_ready, 1)

            def normalise(b):
                if b == 0:
                    act.wait_ge(rstd_ready, 3)
                ins = act.activation(rows[:, b, :], acc[:, b, :], ACT.Identity, scale=rstd_rms[:, b:b + 1],
                                     bias=shift[:, b:b + 1])
                if b == HALF - 1:
                    ins.then_inc(rows_ready, 1)

            def normalise_last(i):
                act.wait_ge(rstd_ready, 4 + i + 1)
                for b in range(HALF * i, HALF * (i + 1)):
                    ins = act.activation(rows[:, b, :], acc[:, b, :], ACT.Identity, scale=rstd[:, 0, b:b + 1],
                                         bias=shift[:, b:b + 1])
                ins.then_inc(rows_ready, 1)

            def exponentials(s, i):
                act.wait_ge(max_ready, 2 * s + i + 1)
                for t in range(HALF):
                    b = HALF * i + t
                    ins = act.activation(probs[:, b, :], probs[:, b, :], ACT.Exp, bias=neg_max[:, b:b + 1],
                                         accum_out=sums[:, b:b + 1])
                ins.then_inc(exp_done, 1)

            def copy_probs_t(s, banks=TO):
                act.wait_ge(probs_turned, 2 * s + 1)
                act.copy(probs_t[:, half(0), :], tiles(banks[0])).then_inc(probs_t0_copied, 1)

            def split_out(s, j, halves=(0, 1)):
                for i in halves:
                    act.wait_ge(pv_done, 2 * s + i + 1)
                    act.copy(ot[0][:, cols(2 * j + i, BANK)], TO[i][:, :]).then_inc(ot_hi_ready, 1)

            def split_weights(piece, g):
                act.wait_ge(raw_loaded[piece], 16 * (g + 2))
                act.copy(w[0][:, piece, :], raw[:, piece, :]).then_inc(w_hi_ready[piece], 1)

            def copy_qk(g, j, k, done=None):
                n = 4 * (PAIR * g + j) + (k if done is None else done)
                act.wait_ge(qk_done, n + 1)
                act.copy((qt, kt)[k // 2][:, cols(k % 2, BANK)], QK[k % 2][:, :]).then_inc(qk_copied, 1)

            def copy_v(g, b):
                act.wait_ge(v_done, B * g + b + 1)
                act.copy(v[:, b, :], VO[b % 2][:, 0:PAIR * P]).then_inc(v_copied, 1)

            def group(g, last=False):
                exponentials(PAIR * g, 0)
                copy_qk(g, 0, 0)
                exponentials(PAIR * g, 1)
                copy_qk(g, 0, 1)
                act.wait_ge(qk_done, 8 * g)
                split_weights(QKB, g)
                copy_qk(g, 0, 2)
                copy_qk(g, 0, 3)
                copy_probs_t(PAIR * g)
                split_out(PAIR * g, 1)
                copy_v(g, 0)
                exponentials(PAIR * g + 1, 0)
                copy_v(g, 1)
                copy_v(g, 2)
                exponentials(PAIR * g + 1, 1)
                for b in range(3, B):
                    copy_v(g, b)
                    if b == 5 and not last:
                        act.wait_ge(qk_done, 8 * g + 4)
                        split_weights(QKA, g + 1)
                copy_probs_t(PAIR * g + 1)
                if not last:
                    act.wait_ge(v_done, B * (g + 1))
                    split_weights(WV, g + 1)
                if last:
                    for k in range(4):
                        copy_qk(g, 1, k)
                    exponentials(HEADS, 0)
                    exponentials(HEADS, 1)
                    act.wait_ge(ffn_loaded, 48)
                    act.copy(ffn[0][:, 0:ffn_cols], ffn_raw[:, :]).then_inc(ffn_hi_ready, 1)
                act.wait_ge(out_done, B * (g + 1))
                split_weights(WO, g)
                if not last:
                    for k in range(4):
                        copy_qk(g, 1, k)
                split_out(PAIR * g + 1, 0)

            def copy_qkv(i, part):
                act.wait_ge(qkv_done, 3 * i + part + 1)
                act.activation((qt, kt, vt_a)[part][:, cols(i, BANK)], QK[(3 * i + part) % 2][:, :], ACT.Identity,
                               bias=b_qkv_cols[:, part:part + 1]).then_inc(qkv_copied, 1)

            def split_context(c):
                act.wait_ge(raw_loaded[c], 16)
                act.copy(ct[0][:, c, :], raw[:, c, :]).then_inc(ct_hi_ready, 1)

            act.wait_ge(raw_qkv_loaded, 16)
            act.copy(ot[0][:, QKV_COLS], raw_a[:, QKV_COLS]).then_inc(w_qkv_hi_ready, 1)
            split_rows(0, 0)
            act.wait_ge(raw_o_loaded, 16)
            act.copy(ot[0][:, OUT_COLS], raw_a[:, OUT_COLS]).then_inc(w_o_hi_ready, 1)
            act.wait_ge(small_loaded, 48)
            copy_qkv(0, 0)
            split_context(0)
            copy_qkv(0, 1)
            split_context(1)
            copy_qkv(0, 2)
            split_rows(0, 1)
            split_context(2)
            copy_qkv(1, 0)
            split_context(3)
            exponentials(0, 0)
            split_weights(QKA, 0)
            copy_qkv(1, 1)
            split_weights(WV, 0)
            copy_qkv(1, 2)
            copy_probs_t(0)
            exponentials(0, 1)
            copy_qk(0, 0, 2, 0)
            split_out(0, 0, (0,))
            copy_qk(0, 0, 3, 1)
            copy_v(0, 0)
            split_out(0, 0, (1,))
            copy_v(0, 1)
            split_weights(WO, 0)
            copy_v(0, 2)
            normalise(0)
            copy_v(0, 3)
            normalise(1)
            normalise(2)
            copy_v(0, 4)
            normalise(3)
            for b in range(5, B):
                copy_v(0, b)
            split_rows(1, 0)
            split_rows(1, 1)
            split_weights(QKB, 0)
            act.wait_ge(v_done, B)
            split_weights(WV, 1)
            copy_qk(0, 0, 0, 2)
            copy_qk(0, 0, 1, 3)
            act.wait_ge(qk_done, 4)
            split_weights(QKA, 1)
            act.wait_ge(scores_done, 4)
            copy_qk(0, 1, 0)
            exponentials(1, 0)
            exponentials(1, 1)
            for k in range(1, 4):
                copy_qk(0, 1, k)
            copy_probs_t(1)
            split_out(1, 0)
            with act.Fori(1, GROUPS - 1) as g:
                group(g)
            group(GROUPS - 1, last=True)
            copy_probs_t(HEADS, QK)
            split_out(HEADS, 1)
            act.wait_ge(ffn_lo_ready, 1)
            normalise_last(0)
            split_rows(2, 0)
            normalise_last(1)
            split_rows(2, 1)
            for i in range(2):
                act.wait_ge(logits_ready, i + 1)
                act.activation(gates[:, half(i), :], logits[:, half(i), :], ACT.Exp).then_inc(gates_exp, 1)
                act.wait_ge(mid_turned, i + 1)
                act.copy(ot[0][:, cols(i, BANK)], TO[i][:, :]).then_inc(mid_hi_ready, 1)

        @block.vector
        def _(dve):
            def add_out(n, b, banks=None):
                dve.wait_ge(out_done, B * n + b + 1)
                dve.tensor_tensor(acc[:, b, :], (banks or VO * HALF)[b][:, :], acc[:, b, :], ALU.add).then_inc(out_added, 1)

            def row_stats(layer, b):
                if layer == 0:
                    dve.wait_ge(x_loaded[b], 16)
                else:
                    dve.wait_ge(out_added, (0, 0, B * GROUPS)[layer] + b + 1)
                dve.bn_stats(stats[:, b, :], acc[:, b, :]).then_inc(stats_step, 1)

            spread_steps = [0]

            def spread_chained(ins):
                spread_steps[0] += 1
                ins.then_inc(spread_step, 1)
                dve.wait_ge(spread_step, spread_steps[0])

            def spreads(layer, i):
                h = half(i)
                var = mean_var[:, h, 1]
                dve.wait_ge(stats_step, B * layer + HALF * (i + 1))
                for b in range(HALF * i, HALF * (i + 1)):
                    ins = dve.bn_aggr(mean_var[:, b, :], stats[:, b, :])
                spread_chained(ins)
                dve.tensor_scalar(neg_mean[:, h], mean_var[:, h, 0], -1.0, None, ALU.mult)
                ins = dve.tensor_scalar(spread[:, 0, h], var, EPS, None, ALU.add)
                if layer == 1:
                    spread_chained(ins)
                    spread_chained(dve.reciprocal(spread[:, 1, h], spread[:, 0, h]))
                    spread_chained(dve.tensor_tensor(spread[:, 1, h], spread[:, 1, h], var, ALU.mult))
                    ins = dve.tensor_scalar(spread[:, 1, h], spread[:, 1, h], EPS, None, ALU.add)
                ins.then_inc(spread_ready, 1)

            def normalise(i):
                dve.wait_ge(rstd_ready, i + 1)
                for b in range(HALF * i, HALF * (i + 1)):
                    ins = dve.tensor_scalar(rows[:, b, :], acc[:, b, :], mean_var[:, b, 0:1], rstd[:, 0, b:b + 1],
                                            ALU.subtract, ALU.mult)
                ins.then_inc(rows_ready, 1)

            def normalise_both():
                dve.wait_ge(rstd_ready, 4)
                for b in range(HALF, B):
                    ins = dve.tensor_scalar(rows[:, b, :], acc[:, b, :], rstd_rms[:, b:b + 1], shift[:, b:b + 1],
                                            ALU.mult, ALU.add)
                ins.then_inc(rows_ready, 1)

            def add_normalised(i):
                h = half(i)
                dve.wait_ge(rstd_ready, 2 + i + 1)
                dve.tensor_scalar(gain[:, h], rstd[:, 0, h], 1.0, None, ALU.add)
                dve.tensor_tensor(offset[:, h], neg_mean[:, h], rstd[:, 0, h], ALU.mult).then_inc(norm_step, 1)
                dve.wait_ge(norm_step, i + 1)
                dve.wait_ge(rows_ready, 2 + i + 1)
                for b in range(HALF * i, HALF * (i + 1)):
                    ins = dve.tensor_scalar(acc[:, b, :], acc[:, b, :], gain[:, b:b + 1], offset[:, b:b + 1],
                                            ALU.mult, ALU.add)
                ins.then_inc(residual_added, 1)

            def split_rows(layer, i):
                for c in range(KC):
                    n = KC * i + c
                    dve.wait_ge(xt_hi_ready, 2 * KC * layer + n + 1)
                    of, hi = ROWS_T[n % len(ROWS_T)][:, :], xt[0][:, c, cols(i, BANK)].bitcast(F32)
                    to = xt[1][:, c, cols(i, BANK)]
                    if layer == 1:
                        ins = dve.scalar_tensor_tensor(out=to, in0=of, scalar=ln_w_cols[:, c:c + 1], in1=hi,
                                                       op0=ALU.mult, op1=ALU.subtract)
                    else:
                        ins = dve.tensor_tensor(to, of, hi, ALU.subtract)
                    ins.then_inc(xt_lo_ready, 1)

            def take_scores(s, i, add=True):
                dve.wait_ge(scores_done, 2 * s + i + 1)
                if add:
                    if i == 0:
                        dve.wait_ge(bias_mask_ready, s)
                    ins = dve.tensor_tensor(probs[:, half(i), :], tiles(SC[i]), bias_mask[:, half(i), :], ALU.add)
                else:
                    ins = dve.tensor_scalar(probs[:, half(i), :], tiles(SC[i]), SCORE_SCALE, None, ALU.mult)
                ins.then_inc(scores_biased, 1)

            def maxima(s, i):
                dve.wait_ge(scores_biased, 2 * s + i + 1)
                dve.tensor_reduce(neg_max[:, half(i)], probs[:, half(i), :], AX.X, ALU.max,
                                  negate=True).then_inc(max_ready, 1)

            def normalise_probs(s, i, masked=True):
                dve.wait_ge(exp_done, 2 * s + i + 1)
                dve.reciprocal(inv[:, half(i)], sums[:, half(i)]).then_inc(inv_ready, 1)
                dve.wait_ge(inv_ready, 2 * s + i + 1)
                scale = inv
                if masked:
                    dve.tensor_tensor(row_scale[:, half(i)], inv[:, half(i)], has_key[:, half(i)],
                                      ALU.mult).then_inc(scale_ready, 1)
                    dve.wait_ge(scale_ready, 2 * s - 2 + i + 1)
                    scale = row_scale
                dve.tensor_tensor(probs[:, half(i), :], probs[:, half(i), :],
                                  scale[:, half(i)].unsqueeze(2).to_broadcast([P, HALF, P]),
                                  ALU.mult).then_inc(probs_ready, 1)

            def copy_probs_t(s, banks=TO):
                dve.wait_ge(probs_turned, 2 * s + 2)
                dve.tensor_copy(probs_t[:, half(1), :], tiles(banks[1])).then_inc(probs_t1_copied, 1)

            def split_out(s, j, halves=(0, 1)):
                for i in halves:
                    dve.wait_ge(ot_hi_ready, 2 * s + i + 1)
                    c = cols(2 * j + i, BANK)
                    dve.tensor_tensor(ot[1][:, c], TO[i][:, :], ot[0][:, c].bitcast(F32),
                                      ALU.subtract).then_inc(ot_lo_ready, 1)

            def split_weights(piece, g):
                dve.wait_ge(w_hi_ready[piece], g + 1)
                dve.tensor_tensor(w[1][:, piece, :], raw[:, piece, :], w[0][:, piece, :].bitcast(F32),
                                  ALU.subtract).then_inc(w_lo_ready[piece], 1)

            def group(g, last=False):
                normalise_probs(PAIR * g, 0)
                normalise_probs(PAIR * g, 1)
                split_weights(QKB, g)
                copy_probs_t(PAIR * g)
                for i in range(2):
                    take_scores(PAIR * g + 1, i)
                for i in range(2):
                    maxima(PAIR * g + 1, i)
                split_out(PAIR * g, 1)
                for i in range(2):
                    normalise_probs(PAIR * g + 1, i)
                if not last:
                    split_weights(QKA, g + 1)
                copy_probs_t(PAIR * g + 1)
                if last:
                    for i in range(2):
                        take_scores(HEADS, i)
                    for i in range(2):
                        maxima(HEADS, i)
                for b in range(B):
                    if last and b in (2, 5):
                        normalise_probs(HEADS, b // 4)
                    add_out(g, b)
                if not last:
                    split_weights(WV, g + 1)
                split_weights(WO, g)
                split_out(PAIR * g + 1, 0)
                if not last:
                    for i in range(2):
                        take_scores(PAIR * g + 2, i)
                    for i in range(2):
                        maxima(PAIR * g + 2, i)

            for b in range(HALF):
                row_stats(0, b)
            spreads(0, 0)
            normalise(0)
            dve.wait_ge(w_qkv_hi_ready, 1)
            dve.tensor_tensor(ot[1][:, QKV_COLS], raw_a[:, QKV_COLS], ot[0][:, QKV_COLS].bitcast(F32),
                              ALU.subtract).then_inc(w_qkv_lo_ready, 1)
            split_rows(0, 0)
            for b in range(HALF, B):
                row_stats(0, b)
            spreads(0, 1)
            normalise(1)
            split_rows(0, 1)

            def copy_values(i):
                dve.wait_ge(values_turned, i + 1)
                dve.tensor_copy(vt_tiles[:, cols(i, BANK)], VO[i][:, :]).then_inc(values_copied, 1)

            def add_b_o(i):
                if i == 0:
                    dve.wait_ge(small_loaded, 48)
                for b in range(HALF * i, HALF * (i + 1)):
                    dve.tensor_tensor(acc[:, b, :], acc[:, b, :], b_o_rows, ALU.add).then_inc(bo_added, 1)

            take_scores(0, 0, add=False)
            maxima(0, 0)
            copy_values(0)
            add_b_o(0)
            normalise_probs(0, 0, masked=False)
            split_weights(QKA, 0)
            take_scores(0, 1, add=False)
            maxima(0, 1)
            copy_values(1)
            split_weights(WV, 0)
            normalise_probs(0, 1, masked=False)
            split_out(0, 0, (0,))
            copy_probs_t(0)
            dve.wait_ge(bo_added, HALF)
            for b in range(HALF):
                add_out(0, b, OWN_OUT)
            add_b_o(1)
            split_out(0, 0, (1,))
            for b in range(HALF):
                row_stats(1, b)
            spreads(1, 0)
            dve.wait_ge(bo_added, B)
            for b in range(HALF, B):
                add_out(0, b, OWN_OUT)
            for b in range(HALF, B):
                row_stats(1, b)
            spreads(1, 1)
            add_normalised(0)
            normalise_both()
            split_rows(1, 0)
            split_rows(1, 1)
            dve.wait_ge(mask_loaded, 16)
            dve.tensor_scalar(mask_add[:, :, :], mask_raw[:, :, :], -1.0, -MASKED, ALU.add,
                              ALU.mult).then_inc(mask_ready, 1)
            split_weights(QKB, 0)
            dve.tensor_reduce(has_key[:, :], mask_raw[:, :, :], AX.X, ALU.max).then_inc(mask_step, 1)
            for i in range(2):
                take_scores(1, i)
            for i in range(2):
                maxima(1, i)
            split_weights(WV, 1)
            dve.wait_ge(mask_step, 1)
            for i in range(2):
                normalise_probs(1, i)
            split_weights(QKA, 1)
            add_normalised(1)
            copy_probs_t(1)
            split_out(1, 0)
            for i in range(2):
                take_scores(2, i)
            for i in range(2):
                maxima(2, i)
            split_weights(WO, 0)
            dve.wait_ge(residual_added, 2)
            with dve.Fori(1, GROUPS - 1) as g:
                group(g)
            group(GROUPS - 1, last=True)
            copy_probs_t(HEADS, QK)
            split_out(HEADS, 1)
            for b in range(HALF):
                add_out(GROUPS, b, LAST_OUT)
            for b in range(HALF):
                row_stats(2, b)
            spreads(2, 0)
            for b in range(HALF, B):
                add_out(GROUPS, b, LAST_OUT)
            for b in range(HALF, B):
                row_stats(2, b)
            spreads(2, 1)
            split_rows(2, 0)
            split_rows(2, 1)
            steps = [0]

            def chained(ins):
                steps[0] += 1
                ins.then_inc(route_step, 1)
                dve.wait_ge(route_step, steps[0])

            def route(i):
                h = half(i)
                dve.wait_ge(routed_done, HALF * (i + 1))
                for n in range(2):
                    tile_pair = VO[n][:, :].rearrange("p (t n) -> p t n", t=2)[:, :, NE * NR:NE * NR + NE]
                    ins = dve.tensor_copy(rank[:, HALF * i + 2 * n:HALF * i + 2 * n + 2, :], tile_pair)
                    chained(ins)
                chained(dve.tensor_reduce(top[:, h], rank[:, h, :], AX.X, ALU.max))
                dve.tensor_tensor(logits[:, h, :], rank[:, h, :], top[:, h].unsqueeze(2).to_broadcast([P, HALF, NE]),
                                  ALU.subtract).then_inc(logits_ready, 1)
                dve.wait_ge(gates_exp, i + 1)
                flat = gates[:, h, :].rearrange("p t e -> p (t e)")
                others = gates[:, h, :].unsqueeze(2).to_broadcast([P, HALF, NE, NE])
                own = flat.unsqueeze(2).to_broadcast([P, HALF * NE, NE]).rearrange("p (t e) j -> p t e j", e=NE)
                beats4 = beats[:, :, :].rearrange("p (t e) j -> p t e j", e=NE)
                ties4 = ties[:, :, :].rearrange("p (t e) j -> p t e j", e=NE)
                before = earlier[:, :, :].unsqueeze(1).to_broadcast([P, HALF, NE, NE])
                chained(dve.tensor_tensor(beats4, others, own, ALU.is_gt))
                chained(dve.tensor_tensor(ties4, others, own, ALU.is_equal))
                chained(dve.tensor_tensor(ties4, ties4, before, ALU.mult))
                chained(dve.tensor_tensor(beats[:, :, :], beats[:, :, :], ties[:, :, :], ALU.add))
                chained(dve.tensor_reduce(rank[:, h, :].rearrange("p t e -> p (t e)"), beats[:, :, :], AX.X, ALU.add))
                chained(dve.scalar_tensor_tensor(out=logits[:, h, :], in0=rank[:, h, :], scalar=1.5,
                                                 in1=gates[:, h, :], op0=ALU.is_lt, op1=ALU.mult))
                chained(dve.tensor_reduce(top_sum[:, h], logits[:, h, :], AX.X, ALU.add))
                chained(dve.reciprocal(top[:, h], top_sum[:, h]))
                chained(dve.scalar_tensor_tensor(out=rank[:, h, :], in0=logits[:, h, :], scalar=LORA_SCALE,
                                                 in1=top[:, h].unsqueeze(2).to_broadcast([P, HALF, NE]),
                                                 op0=ALU.mult, op1=ALU.mult))
                for t in range(HALF):
                    b = HALF * i + t
                    mids = VO[t // 2][:, ROUTED * (t % 2):ROUTED * (t % 2) + NE * NR].rearrange("p (e r) -> p e r", e=NE)
                    ins = dve.tensor_tensor(probs[:, b, :].rearrange("p (e r) -> p e r", e=NE), mids,
                                            rank[:, b, :].unsqueeze(2).to_broadcast([P, NE, NR]), ALU.mult)
                ins.then_inc(mid_ready, 1)

            def split_mid(i):
                dve.wait_ge(mid_hi_ready, i + 1)
                dve.tensor_tensor(ot[1][:, cols(i, BANK)], TO[i][:, :], ot[0][:, cols(i, BANK)].bitcast(F32),
                                  ALU.subtract).then_inc(mid_lo_ready, 1)

            def results(i):
                for t in range(HALF):
                    b = HALF * i + t
                    dve.wait_ge(ffn_done, b + 1)
                    dve.tensor_tensor(acc[:, b, :], (QK + SC)[t][:, :], acc[:, b, :], ALU.add).then_inc(result_ready, 1)

            dve.wait_ge(consts_ready, 1)
            route(0)
            split_mid(0)
            results(0)
            route(1)
            split_mid(1)
            results(1)


def kernel(x, ctx_4096, mask_BxSxS2_bk0, L0_attn_Wqkv, L0_attn_bqkv, L0_attn_Wo, L0_attn_bo,
           L0_xattn_position_bias, L0_xattn_ln_weight, L0_xattn_w_q, L0_xattn_w_k, L0_xattn_w_v, L0_xattn_w_out,
           L0_ffn_base_W, L0_ffn_router_W, L0_ffn_lora_A, L0_ffn_lora_B):
    import numpy as np
    import concourse.bacc as bacc
    from concourse.bass_utils import run_bass_kernel_spmd

    def chunked(a):
        a = np.asarray(a)
        return a.reshape(KC, P, a.shape[1]).transpose(1, 0, 2).reshape(P, KC * a.shape[1])

    f = np.float32
    q, k, v = (np.asarray(a).reshape(GROUPS, PAIR, P, KC, P) for a in (L0_xattn_w_q, L0_xattn_w_k, L0_xattn_w_v))
    pieces = np.empty((GROUPS, 4, P, PIECE), f)
    for j, piece in ((0, QKA), (1, QKB)):
        pieces[:, piece] = np.stack([a[:, j].transpose(0, 3, 2, 1) for a in (q, k)], axis=2).reshape(GROUPS, P, PIECE)
    pieces[:, WV] = v.transpose(0, 4, 3, 1, 2).reshape(GROUPS, P, PIECE)
    pieces[:, WO] = np.asarray(L0_xattn_w_out).T.reshape(GROUPS, PAIR, P, C).transpose(0, 2, 1, 3).reshape(
        GROUPS, P, PIECE)
    routed = np.zeros((C, ROUTED), f)
    routed[:, 0:NE * NR] = np.asarray(L0_ffn_lora_A).transpose(1, 0, 2).reshape(C, NE * NR)
    routed[:, NE * NR:NE * NR + NE] = np.asarray(L0_ffn_router_W).T
    arrays = {
        "x": np.asarray(x).transpose(1, 0, 2),
        "ctx_t": np.asarray(ctx_4096).reshape(T, KC, P).transpose(2, 1, 0),
        "mask": np.asarray(mask_BxSxS2_bk0).transpose(1, 0, 2),
        "w_qkv": chunked(L0_attn_Wqkv),
        "b_qkv": np.asarray(L0_attn_bqkv).reshape(3, P).T,
        "w_o": np.asarray(L0_attn_Wo),
        "b_o": np.asarray(L0_attn_bo),
        "ln_w": np.asarray(L0_xattn_ln_weight).reshape(KC, P).T,
        "pos_bias": np.asarray(L0_xattn_position_bias).reshape(GROUPS, PAIR, P, P).transpose(0, 2, 1, 3),
        "weights": pieces,
        "w_base": chunked(np.asarray(L0_ffn_base_W).T),
        "w_routed": chunked(routed),
        "w_lora_b": np.asarray(L0_ffn_lora_B).reshape(NE * NR, C),
    }
    nc = bacc.Bacc("TRN2", target_bir_lowering=False, num_devices=1)
    sent, args = {}, []
    for name, a in arrays.items():
        a = np.ascontiguousarray(a)
        sent[f"in_{name}"] = a
        args.append(nc.dram_tensor(f"in_{name}", a.shape, mybir.dt.from_np(a.dtype), kind="ExternalInput").ap())
    args.append(nc.dram_tensor("out_rows", (P, B, C), F32, kind="ExternalOutput").ap())
    decoder_kernel(nc, *args)
    result = run_bass_kernel_spmd(nc, [sent], core_ids=[0])
    return np.ascontiguousarray(result.results[0]["out_rows"].transpose(1, 0, 2))
```

```python
from contextlib import ExitStack

import concourse.bass as bass
from concourse import mybir

ALU = mybir.AluOpType
ACT = mybir.ActivationFunctionType
AX = mybir.AxisListType
F32 = mybir.dt.float32
F32R = mybir.dt.float32r

P = 128
B = 8
C = 512
KC = C // P
T = B * P
HEADS = 32
PAIR = 2
GROUPS = HEADS // PAIR
HALF = B // 2
BANK = 512
NE, NR = 8, 16
ROUTED = 256
QKV_COLS, OUT_COLS = slice(0, KC * 3 * P), slice(KC * 3 * P, KC * 3 * P + C)
PIECE = PAIR * C
QKA, WV, WO, QKB = range(4)
EPS = 1e-5
MASKED = -1e30
SCORE_SCALE = float(P) ** -0.5
LORA_SCALE = 32 / 16


def decoder_kernel(nc, x, ctx_t, mask, w_qkv, b_qkv, w_o, b_o, ln_w, pos_bias, weights, w_base, w_routed, w_lora_b,
                   out):
    with ExitStack() as ctx:
        def sb(name, shape, dt=F32):
            return ctx.enter_context(nc.sbuf_tensor(name, shape, dt))

        def sem(name):
            return ctx.enter_context(nc.semaphore(name))

        acc = sb("acc", [P, B, C])
        rows = sb("rows", [P, B, C])
        xt = [sb("xt_hi", [P, KC, T], F32R), sb("xt_lo", [P, KC, T], F32R)]
        ct = [sb("ct_hi", [P, KC, T], F32R), sb("ct_lo", [P, KC, T], F32R)]
        raw = sb("raw", [P, 4, PIECE])
        w = [sb("w_hi", [P, 4, PIECE], F32R), sb("w_lo", [P, 4, PIECE], F32R)]
        raw_a = sb("raw_a", [P, KC * 3 * P + C])
        ot = [sb("ot_hi", [P, PAIR * T], F32R), sb("ot_lo", [P, PAIR * T], F32R)]
        qt = sb("qt", [P, T])
        kt = sb("kt", [P, T])
        v = sb("v", [P, B, PAIR * P])
        probs = sb("probs", [P, B, P])
        probs_t = sb("probs_t", [P, B, P])
        bias = sb("bias", [P, PAIR, P])
        bias_mask = sb("bias_mask", [P, B, P])
        mask_add = sb("mask_add", [P, B, P])
        mask_raw = sb("mask_raw", [P, B, P], mask.dtype)
        has_key = sb("has_key", [P, B])
        b_o_rows = bias_mask[:, 0:C // P, :].rearrange("p b n -> p (b n)")
        b_qkv_cols = sb("b_qkv_cols", [P, 3])
        ln_w_cols = sb("ln_w_cols", [P, KC])
        ident = sb("ident", [P, P])
        earlier = sb("earlier", [P, NE, NE])
        minus_half = sb("minus_half", [P, 2, HALF])
        stats = sb("stats", [P, B, 6])
        mean_var = sb("mean_var", [P, B, 2])
        spread = sb("spread", [P, 2, B])
        rstd = sb("rstd", [P, 2, B])
        rstd_rms = sb("rstd_rms", [P, B])
        neg_mean = sb("neg_mean", [P, B])
        gain = sb("gain", [P, B])
        offset = sb("offset", [P, B])
        shift = sb("shift", [P, B])
        neg_max = sb("neg_max", [P, B])
        sums = sb("sums", [P, B])
        inv = sb("inv", [P, B])
        row_scale = sb("row_scale", [P, B])
        logits = sb("logits", [P, B, NE])
        gates = sb("gates", [P, B, NE])
        beats, ties = (probs_t[:, n:n + 2, :].rearrange("p b (e j) -> p (b e) j", j=NE) for n in (0, 2))
        rank = sb("rank", [P, B, NE])
        top = sb("top", [P, B])
        top_sum = sb("top_sum", [P, B])

        ot_last = [t[:, 0:PAIR, :].rearrange("p c n -> p (c n)") for t in xt]
        WO_LAST = QKA
        w_qkv_s = [t[:, QKV_COLS].rearrange("p (c n) -> p c n", c=KC) for t in ot]
        w_o_s = [t[:, OUT_COLS] for t in ot]
        vt_a = v[:, :, :].rearrange("p b n -> p (b n)")[:, 0:T]
        vt_tiles = v[:, :, :].rearrange("p b n -> p (b n)")[:, T:2 * T]
        ffn_cols = KC * C + KC * ROUTED + C
        ffn_raw = rows[:, :, :].rearrange("p b n -> p (b n)")[:, 0:ffn_cols]
        ffn = [t[:, :, :].rearrange("p c n -> p (c n)") for t in ct]
        base_s = [t[:, 0:KC * C].rearrange("p (c n) -> p c n", c=KC) for t in ffn]
        routed_s = [t[:, KC * C:KC * (C + ROUTED)].rearrange("p (c n) -> p c n", c=KC) for t in ffn]
        lora_b_s = [t[:, KC * (C + ROUTED):ffn_cols] for t in ffn]

        bank = [ctx.enter_context(nc.psum_tensor(f"bank{i}", [P, BANK], F32)) for i in range(8)]
        QK, SC, TO, VO = bank[0:2], bank[2:4], bank[4:6], bank[6:8]
        ROWS_T = (SC + TO, SC + TO, TO + QK)
        OWN_OUT = (SC + QK) * 2
        LAST_OUT = (SC + QK + VO) + SC
        BASE = SC + QK

        x_loaded = [sem(f"x_loaded{b}") for b in range(B)]
        raw_loaded = [sem(f"raw_loaded{p}") for p in range(4)]
        raw_qkv_loaded = sem("raw_qkv_loaded")
        raw_o_loaded = sem("raw_o_loaded")
        small_loaded = sem("small_loaded")
        mask_loaded = sem("mask_loaded")
        bias_loaded = sem("bias_loaded")
        ffn_loaded = sem("ffn_loaded")
        stored = sem("stored")
        ident_ready = sem("ident_ready")
        const_step = sem("const_step")
        consts_ready = sem("consts_ready")
        stats_step = sem("stats_step")
        spread_step = sem("spread_step")
        spread_ready = sem("spread_ready")
        rstd_step = sem("rstd_step")
        rstd_ready = sem("rstd_ready")
        norm_step = sem("norm_step")
        residual_added = sem("residual_added")
        rows_ready = sem("rows_ready")
        rows_ready_v = sem("rows_ready_v")
        rows_t_done = sem("rows_t_done")
        xt_hi_ready = sem("xt_hi_ready")
        xt_lo_ready = sem("xt_lo_ready")
        ct_hi_ready = sem("ct_hi_ready")
        ct_lo_ready = sem("ct_lo_ready")
        w_qkv_hi_ready = sem("w_qkv_hi_ready")
        w_qkv_lo_ready = sem("w_qkv_lo_ready")
        w_o_hi_ready = sem("w_o_hi_ready")
        w_o_lo_ready = sem("w_o_lo_ready")
        w_hi_ready = [sem(f"w_hi_ready{p}") for p in range(4)]
        w_lo_ready = [sem(f"w_lo_ready{p}") for p in range(4)]
        ffn_hi_ready = sem("ffn_hi_ready")
        ffn_lo_ready = sem("ffn_lo_ready")
        qkv_done = sem("qkv_done")
        qkv_copied = sem("qkv_copied")
        values_turned = sem("values_turned")
        values_copied = sem("values_copied")
        bo_added = sem("bo_added")
        mask_step = sem("mask_step")
        mask_ready = sem("mask_ready")
        bias_mask_ready = sem("bias_mask_ready")
        qk_done = sem("qk_done")
        qk_copied = sem("qk_copied")
        v_done = sem("v_done")
        v_copied = sem("v_copied")
        scores_done = sem("scores_done")
        scores_biased = sem("scores_biased")
        max_ready = sem("max_ready")
        exp_done = sem("exp_done")
        inv_ready = sem("inv_ready")
        scale_ready = sem("scale_ready")
        probs_ready = sem("probs_ready")
        probs_turned = sem("probs_turned")
        probs_t0_copied = sem("probs_t0_copied")
        probs_t1_copied = sem("probs_t1_copied")
        pv_done = sem("pv_done")
        ot_hi_ready = sem("ot_hi_ready")
        ot_lo_ready = sem("ot_lo_ready")
        out_done = sem("out_done")
        out_added = sem("out_added")
        routed_done = sem("routed_done")
        route_step = sem("route_step")
        logits_ready = sem("logits_ready")
        gates_exp = sem("gates_exp")
        mid_ready = sem("mid_ready")
        mid_turned = sem("mid_turned")
        mid_hi_ready = sem("mid_hi_ready")
        mid_lo_ready = sem("mid_lo_ready")
        ffn_done = sem("ffn_done")
        result_ready = sem("result_ready")

        def half(i):
            return slice(HALF * i, HALF * (i + 1))

        def spans(layer, i):
            return 2 * layer + i + 2

        def cols(i, n=P):
            return slice(n * i, n * (i + 1))

        def tiles(bank_ap):
            return bank_ap[:, :].rearrange("p (b n) -> p b n", b=HALF)

        block = ctx.enter_context(nc.Block())

        @block.sync
        def _(sp):
            for b in range(HALF):
                sp.dma_start(acc[:, b, :], x[:, b, :]).then_inc(x_loaded[b], 16)
            sp.dma_start(raw_a[:, QKV_COLS], w_qkv).then_inc(raw_qkv_loaded, 16)
            for b in range(HALF, B):
                sp.dma_start(acc[:, b, :], x[:, b, :]).then_inc(x_loaded[b], 16)
            sp.dma_start(raw_a[:, OUT_COLS], w_o).then_inc(raw_o_loaded, 16)
            sp.dma_start(b_qkv_cols[:, :], b_qkv).then_inc(small_loaded, 16)
            sp.dma_start(ln_w_cols[:, :], ln_w).then_inc(small_loaded, 16)
            sp.dma_start(b_o_rows, b_o.partition_broadcast(P)).then_inc(small_loaded, 16)
            for c in range(KC):
                sp.dma_start(raw[:, c, :], ctx_t[:, c, :]).then_inc(raw_loaded[c], 16)
            sp.dma_start(mask_raw[:, :, :], mask).then_inc(mask_loaded, 16)
            sp.dma_start(bias[:, :, :], pos_bias[0]).then_inc(bias_loaded, 16)

            def load(piece, g):
                sp.dma_start(raw[:, piece, :], weights[g, piece]).then_inc(raw_loaded[piece], 16)

            for piece in range(4):
                sp.wait_ge(ct_lo_ready, piece + 1)
                load(piece, 0)
            for piece in (QKA, WV):
                sp.wait_ge(w_lo_ready[piece], 1)
                load(piece, 1)

            def refill(g, last=False):
                sp.wait_ge(w_lo_ready[QKB], g + 1)
                load(QKB, g + 1)
                sp.wait_ge(bias_mask_ready, PAIR * g + PAIR)
                sp.dma_start(bias[:, :, :], pos_bias[g + 1]).then_inc(bias_loaded, 16)
                if not last:
                    for piece in (QKA, WV):
                        sp.wait_ge(w_lo_ready[piece], g + 2)
                        load(piece, g + 2)
                sp.wait_ge(w_lo_ready[WO], g + 1)
                load(WO, g + 1)

            with sp.Fori(0, GROUPS - 2) as g:
                refill(g)
            refill(GROUPS - 2, last=True)
            n = 0
            for src, width in ((w_base, KC * C), (w_routed, KC * ROUTED), (w_lora_b, C)):
                sp.dma_start(ffn_raw[:, n:n + width], src).then_inc(ffn_loaded, 16)
                n += width
            for b in range(B):
                sp.wait_ge(result_ready, b + 1)
                sp.dma_start(out[:, b, :], acc[:, b, :]).then_inc(stored, 16)
            sp.wait_ge(stored, 16 * B)

        @block.gpsimd
        def _(pool):
            step = [0]

            def chained(ins):
                step[0] += 1
                ins.then_inc(const_step, 1)
                pool.wait_ge(const_step, step[0])

            chained(pool.memset(ident[:, :], 0.0))
            pool.affine_select(out=ident[:, :], in_=ident[:, :], compare_op=ALU.not_equal, fill=1.0, base=0,
                               pattern=[[-1, P]], channel_multiplier=1).then_inc(ident_ready, 1)
            chained(pool.memset(earlier[:, :, :], 1.0))
            pool.affine_select(out=earlier[:, :, :], in_=earlier[:, :, :], compare_op=ALU.is_gt, fill=0.0, base=0,
                               pattern=[[1, NE], [-1, NE]], channel_multiplier=0).then_inc(consts_ready, 1)
            chained(pool.memset(minus_half[:, :, :], -0.5))

            rstd_steps = [0]

            def rstd_chained(ins):
                rstd_steps[0] += 1
                ins.then_inc(rstd_step, 1)
                pool.wait_ge(rstd_step, rstd_steps[0])

            def root(layer, h, count):
                n = 2 if layer == 1 else 1
                pool.wait_ge(spread_ready, count)
                ins = pool.tensor_tensor(rstd[:, 0:n, h], spread[:, 0:n, h], minus_half[:, 0:n, 0:h.stop - h.start],
                                         ALU.pow)
                if layer == 1:
                    rstd_chained(ins)
                    ins = pool.tensor_tensor(rstd_rms[:, h], rstd[:, 0, h], rstd[:, 1, h], ALU.mult)
                if layer:
                    scale = rstd_rms if layer == 1 else rstd[:, 0, :]
                    rstd_chained(ins)
                    ins = pool.tensor_tensor(shift[:, h], neg_mean[:, h], scale[:, h], ALU.mult)
                ins.then_inc(rstd_ready, 1)

            root(0, slice(0, 2), 1)
            root(0, slice(2, HALF), 2)
            root(0, half(1), spans(0, 1))
            pool.wait_ge(w_o_hi_ready, 1)
            pool.tensor_tensor(ot[1][:, OUT_COLS], raw_a[:, OUT_COLS], ot[0][:, OUT_COLS].bitcast(F32),
                               ALU.subtract).then_inc(w_o_lo_ready, 1)
            for c in range(KC):
                pool.wait_ge(ct_hi_ready, c + 1)
                pool.tensor_tensor(ct[1][:, c, :], raw[:, c, :], ct[0][:, c, :].bitcast(F32),
                                   ALU.subtract).then_inc(ct_lo_ready, 1)
            root(1, half(0), spans(1, 0))
            root(1, half(1), spans(1, 1))
            pool.wait_ge(mask_ready, 1)

            def add_mask(g):
                pool.wait_ge(bias_loaded, 16 * (g + 1))
                for j in range(PAIR):
                    pool.wait_ge(scores_biased, 2 * (PAIR * g + j + 1))
                    pool.tensor_tensor(bias_mask[:, :, :], mask_add[:, :, :],
                                       bias[:, j, :].unsqueeze(1).to_broadcast([P, B, P]),
                                       ALU.add).then_inc(bias_mask_ready, 1)

            with pool.Fori(0, GROUPS) as g:
                add_mask(g)
            pool.wait_ge(ffn_hi_ready, 1)
            pool.tensor_tensor(ffn[1][:, 0:ffn_cols], ffn_raw[:, :], ffn[0][:, 0:ffn_cols].bitcast(F32),
                               ALU.subtract).then_inc(ffn_lo_ready, 1)
            root(2, half(0), spans(2, 0))
            root(2, half(1), spans(2, 1))

        @block.tensor
        def _(pe):
            def three_pass(out_ap, pairs, start=True, stop=True):
                n = len(pairs) * 3
                k = 0
                for lhs, rhs in pairs:
                    for a, b in ((0, 0), (0, 1), (1, 0)):
                        ins = pe.matmul(out_ap, lhs[a], rhs[b], start=start and k == 0, stop=stop and k == n - 1)
                        k += 1
                return ins

            def turn_rows(layer, i):
                if i == 0 and layer:
                    pe.wait_ge(out_added, (0, B, B * (GROUPS + 1) - HALF)[layer])
                pe.wait_ge(rows_ready, spans(layer, i))
                if layer + i >= 2:
                    pe.wait_ge(rows_ready_v, 2 * layer + i - 2)
                for c in range(KC):
                    if i:
                        pe.wait_ge(xt_lo_ready, 2 * KC * layer + c + 1)
                    for t in range(HALF):
                        ins = pe.transpose(ROWS_T[layer][c][:, cols(t)],
                                           rows[:, HALF * i + t, cols(c)], ident[:, :])
                    ins.then_inc(rows_t_done, 1)

            def turn_first_rows():
                for k in range(2):
                    pe.wait_ge(rows_ready, k + 1)
                    for c in range(KC):
                        for b in (2 * k, 2 * k + 1):
                            ins = pe.transpose(ROWS_T[0][c][:, cols(b)], rows[:, b, cols(c)], ident[:, :])
                        if k == 1:
                            ins.then_inc(rows_t_done, 1)

            def scores(s, i):
                for t in range(HALF):
                    b = HALF * i + t
                    ins = pe.matmul(SC[i][:, cols(t)], qt[:, cols(b)], kt[:, cols(b)], start=True, stop=True)
                ins.then_inc(scores_done, 1)

            def turn_probs(s, halves=(0, 1)):
                for i in halves:
                    pe.wait_ge(probs_ready, 2 * s + i + 1)
                    for t in range(HALF):
                        ins = pe.transpose(TO[i][:, cols(t)], probs[:, HALF * i + t, :], ident[:, :])
                    ins.then_inc(probs_turned, 1)

            def weigh_values(s, values, halves=(0, 1)):
                for i in halves:
                    pe.wait_ge((probs_t0_copied, probs_t1_copied)[i], s + 1)
                    for t in range(HALF):
                        b = HALF * i + t
                        ins = pe.matmul(TO[i][:, cols(t)], values(b), probs_t[:, b, :], start=True, stop=True)
                    ins.then_inc(pv_done, 1)

            def project_qk(g, j, steps=range(4), done=0):
                piece = (QKA, QKB)[j]
                pe.wait_ge(w_lo_ready[piece], g + 1)
                for k in steps:
                    part, i = k // 2, k % 2
                    if done >= 2 or j or not isinstance(g, int) or g:
                        pe.wait_ge(qk_copied, 4 * (PAIR * g + j) + done - 1)
                    three_pass(QK[i][:, :],
                               [([s[:, piece, cols(KC * part + c)] for s in w],
                                 [s[:, c, cols(i, BANK)] for s in (xt, ct)[part]])
                                for c in range(KC)]).then_inc(qk_done, 1)
                    done += 1

            def project_v(g, some=range(B), first=False):
                pe.wait_ge(w_lo_ready[WV], g + 1)
                for b in some:
                    if b >= 2:
                        pe.wait_ge(v_copied, B * g + b - 1)
                    elif first:
                        pe.wait_ge(values_copied, b + 1)
                    else:
                        pe.wait_ge(out_added, B * g)
                    three_pass(VO[b % 2][:, 0:PAIR * P],
                               [([s[:, c, cols(b)] for s in ct], [s[:, WV, cols(c, PAIR * P)] for s in w])
                                for c in range(KC)]).then_inc(v_done, 1)

            def project_out(g):
                pe.wait_ge(w_lo_ready[WO], g + 1)
                pe.wait_ge(ot_lo_ready, 2 + 2 * PAIR * (g + 1))
                for b in range(B):
                    if b >= 2:
                        pe.wait_ge(out_added, B * (g + 1) + b - 1)
                    else:
                        pe.wait_ge(v_copied, B * (g + 2))
                    three_pass(VO[b % 2][:, :],
                               [([s[:, cols(j * B + b)] for s in ot], [s[:, WO, cols(j, C)] for s in w])
                                for j in range(PAIR)]).then_inc(out_done, 1)

            def head_scores(h):
                pe.wait_ge(qk_copied, 4 * h + 4)
                for i in range(2):
                    pe.wait_ge(scores_biased, 2 * h + i + 1)
                    scores(h + 1, i)

            def turn_head_probs(h):
                pe.wait_ge(ot_lo_ready, 2 * (h + 1))
                turn_probs(h + 1)

            def weigh_head_values(g, j):
                pe.wait_ge(v_copied, B * (g + 1))
                weigh_values(PAIR * g + j + 1, lambda b: v[:, b, cols(j)])

            def group(g, last=False):
                project_qk(g, 0)
                turn_head_probs(PAIR * g - 1)
                head_scores(PAIR * g)
                weigh_head_values(g - 1, 1)
                project_v(g)
                turn_head_probs(PAIR * g)
                if last:
                    project_qk(g, 1)
                    weigh_head_values(g, 0)
                    head_scores(PAIR * g + 1)
                    project_out(g - 1)
                else:
                    project_out(g - 1)
                    project_qk(g, 1)
                    weigh_head_values(g, 0)
                    head_scores(PAIR * g + 1)

            def last_out():
                g = GROUPS - 1

                def part(b, j):
                    return three_pass(LAST_OUT[b][:, :],
                                      [([s[:, cols(j * B + b)] for s in ot_last],
                                        [s[:, WO_LAST, cols(j, C)] for s in w])],
                                      start=(j == 0), stop=(j == 1))

                turn_head_probs(HEADS - 1)
                pe.wait_ge(w_lo_ready[WO], GROUPS)
                pe.wait_ge(scores_biased, 2 * HEADS + 2)
                part(0, 0)
                part(1, 0)
                weigh_head_values(g, 1)
                pe.wait_ge(qk_copied, 4 * HEADS)
                part(2, 0)
                for b in range(B):
                    if b % HALF == 0:
                        pe.wait_ge(ot_lo_ready, 2 * HEADS + 1 + b // HALF)
                    if b >= HALF:
                        pe.wait_ge(out_added, B * GROUPS + max(0, b - 6 + 1))
                    if b >= 3:
                        part(b, 0)
                    part(b, 1).then_inc(out_done, 1)

            def follow_rows(out_ap, lhs, layer, i):
                for c in range(KC):
                    pe.wait_ge(xt_lo_ready, 2 * KC * layer + KC * i + c + 1)
                    ins = three_pass(out_ap, [(lhs(c), [s[:, c, cols(i, BANK)] for s in xt])],
                                     start=(c == 0), stop=(c == KC - 1))
                return ins

            def project_qkv(i, parts=(0, 1, 2)):
                for part in parts:
                    n = 3 * i + part
                    if n >= 2:
                        pe.wait_ge(qkv_copied, n - 1)
                    follow_rows(QK[n % 2][:, :], lambda c: [s[:, c, cols(part)] for s in w_qkv_s],
                                0, i).then_inc(qkv_done, 1)

            def turn_values(i):
                pe.wait_ge(qkv_copied, 3 * (i + 1))
                for t in range(HALF):
                    ins = pe.transpose(VO[i][:, cols(t)], vt_a[:, cols(HALF * i + t)], ident[:, :])
                ins.then_inc(values_turned, 1)

            def own_values(i):
                pe.wait_ge(values_copied, i + 1)
                weigh_values(0, lambda b: vt_tiles[:, cols(b)], (i,))

            def own_out(i):
                pe.wait_ge(ot_lo_ready, i + 1)
                pe.wait_ge(w_o_lo_ready, 1)
                for b in range(HALF * i, HALF * (i + 1)):
                    if i:
                        pe.wait_ge(out_added, b - HALF + 1)
                    elif b >= len(SC):
                        pe.wait_ge(qk_copied, b - len(SC) + 1)
                    three_pass(OWN_OUT[b][:, :], [([s[:, cols(b)] for s in ot], w_o_s)]).then_inc(out_done, 1)

            pe.wait_ge(ident_ready, 1)
            turn_first_rows()
            pe.wait_ge(w_qkv_lo_ready, 1)
            project_qkv(0)
            turn_rows(0, 1)
            turn_values(0)
            project_qkv(1, (0,))
            pe.wait_ge(xt_lo_ready, 2 * KC)
            scores(0, 0)
            project_qkv(1, (1, 2))
            pe.wait_ge(qkv_copied, 5)
            scores(0, 1)
            turn_values(1)
            turn_probs(0, (0,))
            pe.wait_ge(ct_lo_ready, KC)
            pe.wait_ge(qkv_copied, 6)
            project_qk(0, 0, (2,), 0)
            own_values(0)
            project_qk(0, 0, (3,), 1)
            turn_probs(0, (1,))
            own_out(0)
            project_v(0, (0,), first=True)
            own_values(1)
            project_v(0, (1,), first=True)
            own_out(1)
            project_v(0, range(2, B))
            for i in range(2):
                turn_rows(1, i)
                pe.wait_ge(qk_copied, i + 1)
                follow_rows(QK[i][:, :], lambda c: [s[:, QKA, cols(c)] for s in w], 1, i).then_inc(qk_done, 1)
            project_qk(0, 1, (0,), 0)
            head_scores(0)
            project_qk(0, 1, (1, 2, 3), 1)
            turn_head_probs(0)
            weigh_head_values(0, 0)
            head_scores(1)
            with pe.Fori(1, GROUPS - 1) as g:
                group(g)
            group(GROUPS - 1, last=True)
            last_out()

            def routed(i):
                for pair in range(2):
                    for c in range(KC):
                        if pair == 0:
                            pe.wait_ge(xt_lo_ready, 2 * KC * 2 + KC * i + c + 1)
                        for n in range(2):
                            ins = three_pass(VO[n][:, cols(pair, ROUTED)],
                                             [([s[:, c, cols(HALF * i + 2 * pair + n)] for s in xt],
                                               [s[:, c, :] for s in routed_s])], start=(c == 0), stop=(c == KC - 1))
                    ins.then_inc(routed_done, 1)

            def base(i, some):
                for t in some:
                    b = HALF * i + t
                    if i:
                        pe.wait_ge(result_ready, t + 1)
                    elif t >= len(SC):
                        pe.wait_ge(xt_lo_ready, 2 * KC * 3)
                    three_pass(BASE[t][:, :],
                               [([s[:, c, cols(b)] for s in xt], [s[:, c, :] for s in base_s])
                                for c in range(KC)], stop=False)

            def turn_mids(i):
                pe.wait_ge(mid_ready, i + 1)
                for t in range(HALF):
                    ins = pe.transpose(TO[i][:, cols(t)], probs[:, HALF * i + t, :], ident[:, :])
                ins.then_inc(mid_turned, 1)

            def lora(i):
                pe.wait_ge(mid_lo_ready, i + 1)
                for t in range(HALF):
                    b = HALF * i + t
                    three_pass(BASE[t][:, :], [([s[:, cols(b)] for s in ot], lora_b_s)],
                               start=False).then_inc(ffn_done, 1)

            turn_rows(2, 0)
            pe.wait_ge(ffn_lo_ready, 1)
            pe.wait_ge(out_added, B * (GROUPS + 1))
            routed(0)
            base(0, (0,))
            turn_rows(2, 1)
            base(0, (1, 2, 3))
            turn_mids(0)
            routed(1)
            lora(0)
            base(1, (0, 1, 2))
            turn_mids(1)
            base(1, (3,))
            lora(1)

        @block.scalar
        def _(act):
            def split_rows(layer, i):
                for c in range(KC):
                    n = KC * i + c
                    act.wait_ge(rows_t_done, 2 * KC * layer + n + 1)
                    to, of = xt[0][:, c, cols(i, BANK)], ROWS_T[layer][c][:, :]
                    scale = ln_w_cols[:, c:c + 1] if layer == 1 else 1.0
                    act.activation(to, of, ACT.Copy, scale=scale).then_inc(xt_hi_ready, 1)

            def normalise(layer, i, some, last=True):
                act.wait_ge(rstd_ready, spans(layer, i))
                for b in some:
                    scale = rstd_rms[:, b:b + 1] if layer == 1 else rstd[:, 0, b:b + 1]
                    ins = act.activation(rows[:, b, :], acc[:, b, :], ACT.Identity, scale=scale, bias=shift[:, b:b + 1])
                if last:
                    ins.then_inc(rows_ready, 1)

            def exponentials(s, i):
                act.wait_ge(max_ready, 2 * s + i + 1)
                for t in range(HALF):
                    b = HALF * i + t
                    ins = act.activation(probs[:, b, :], probs[:, b, :], ACT.Exp, bias=neg_max[:, b:b + 1],
                                         accum_out=sums[:, b:b + 1])
                ins.then_inc(exp_done, 1)

            def copy_probs_t(s):
                act.wait_ge(probs_turned, 2 * s + 1)
                act.copy(probs_t[:, half(0), :], tiles(TO[0])).then_inc(probs_t0_copied, 1)

            def split_out(s, j, halves=(0, 1), to=ot):
                for i in halves:
                    act.wait_ge(pv_done, 2 * s + i + 1)
                    act.copy(to[0][:, cols(2 * j + i, BANK)], TO[i][:, :]).then_inc(ot_hi_ready, 1)

            def split_weights(piece, g, to=None):
                act.wait_ge(raw_loaded[piece], 16 * (g + 2))
                act.copy(w[0][:, piece if to is None else to, :], raw[:, piece, :]).then_inc(w_hi_ready[piece], 1)

            def copy_qk(g, j, k, done=None):
                n = 4 * (PAIR * g + j) + (k if done is None else done)
                act.wait_ge(qk_done, n + 1)
                act.copy((qt, kt)[k // 2][:, cols(k % 2, BANK)], QK[k % 2][:, :]).then_inc(qk_copied, 1)

            def copy_v(g, b):
                act.wait_ge(v_done, B * g + b + 1)
                act.copy(v[:, b, :], VO[b % 2][:, 0:PAIR * P]).then_inc(v_copied, 1)

            def group(g, last=False):
                exponentials(PAIR * g, 0)
                copy_qk(g, 0, 0)
                exponentials(PAIR * g, 1)
                copy_qk(g, 0, 1)
                act.wait_ge(qk_done, 8 * g)
                split_weights(QKB, g)
                copy_qk(g, 0, 2)
                copy_qk(g, 0, 3)
                copy_probs_t(PAIR * g)
                split_out(PAIR * g, 1)
                copy_v(g, 0)
                exponentials(PAIR * g + 1, 0)
                copy_v(g, 1)
                copy_v(g, 2)
                exponentials(PAIR * g + 1, 1)
                for b in range(3, B):
                    copy_v(g, b)
                    if b == 5:
                        act.wait_ge(qk_done, 8 * g + 4)
                        if last:
                            split_weights(WO, g, WO_LAST)
                        else:
                            split_weights(QKA, g + 1)
                copy_probs_t(PAIR * g + 1)
                if last:
                    for k in range(4):
                        copy_qk(g, 1, k)
                    split_out(PAIR * g + 1, 0, to=ot_last)
                    exponentials(HEADS, 0)
                    exponentials(HEADS, 1)
                    act.wait_ge(ffn_loaded, 48)
                    act.copy(ffn[0][:, 0:ffn_cols], ffn_raw[:, :]).then_inc(ffn_hi_ready, 1)
                else:
                    act.wait_ge(v_done, B * (g + 1))
                    split_weights(WV, g + 1)
                    act.wait_ge(out_done, B * (g + 1))
                    split_weights(WO, g)
                    for k in range(4):
                        copy_qk(g, 1, k)
                    split_out(PAIR * g + 1, 0)

            def copy_qkv(i, part):
                act.wait_ge(qkv_done, 3 * i + part + 1)
                act.activation((qt, kt, vt_a)[part][:, cols(i, BANK)], QK[(3 * i + part) % 2][:, :], ACT.Identity,
                               bias=b_qkv_cols[:, part:part + 1]).then_inc(qkv_copied, 1)

            def split_context(c):
                act.wait_ge(raw_loaded[c], 16)
                act.copy(ct[0][:, c, :], raw[:, c, :]).then_inc(ct_hi_ready, 1)

            act.wait_ge(raw_qkv_loaded, 16)
            act.copy(ot[0][:, QKV_COLS], raw_a[:, QKV_COLS]).then_inc(w_qkv_hi_ready, 1)
            split_rows(0, 0)
            act.wait_ge(raw_o_loaded, 16)
            act.copy(ot[0][:, OUT_COLS], raw_a[:, OUT_COLS]).then_inc(w_o_hi_ready, 1)
            act.wait_ge(small_loaded, 48)
            copy_qkv(0, 0)
            split_context(0)
            copy_qkv(0, 1)
            split_context(1)
            copy_qkv(0, 2)
            split_rows(0, 1)
            split_context(2)
            copy_qkv(1, 0)
            split_context(3)
            exponentials(0, 0)
            split_weights(QKA, 0)
            copy_qkv(1, 1)
            split_weights(WV, 0)
            copy_qkv(1, 2)
            copy_probs_t(0)
            exponentials(0, 1)
            copy_qk(0, 0, 2, 0)
            split_out(0, 0, (0,))
            copy_qk(0, 0, 3, 1)
            copy_v(0, 0)
            split_out(0, 0, (1,))
            copy_v(0, 1)
            split_weights(WO, 0)
            copy_v(0, 2)
            normalise(1, 0, (0,), last=False)
            copy_v(0, 3)
            normalise(1, 0, (1, 2), last=False)
            copy_v(0, 4)
            normalise(1, 0, (3,))
            for b in range(5, B):
                copy_v(0, b)
            split_rows(1, 0)
            normalise(1, 1, (6, 7))
            split_weights(QKB, 0)
            split_rows(1, 1)
            act.wait_ge(v_done, B)
            split_weights(WV, 1)
            copy_qk(0, 0, 0, 2)
            copy_qk(0, 0, 1, 3)
            act.wait_ge(qk_done, 4)
            split_weights(QKA, 1)
            act.wait_ge(scores_done, 4)
            copy_qk(0, 1, 0)
            exponentials(1, 0)
            exponentials(1, 1)
            for k in range(1, 4):
                copy_qk(0, 1, k)
            copy_probs_t(1)
            split_out(1, 0)
            with act.Fori(1, GROUPS - 1) as g:
                group(g)
            group(GROUPS - 1, last=True)
            copy_probs_t(HEADS)
            split_out(HEADS, 1, to=ot_last)
            act.wait_ge(ffn_lo_ready, 1)
            normalise(2, 0, (0, 1))
            split_rows(2, 0)
            normalise(2, 1, (4, 5))
            split_rows(2, 1)
            for i in range(2):
                act.wait_ge(logits_ready, i + 1)
                act.activation(gates[:, half(i), :], logits[:, half(i), :], ACT.Exp).then_inc(gates_exp, 1)
                act.wait_ge(mid_turned, i + 1)
                act.copy(ot[0][:, cols(i, BANK)], TO[i][:, :]).then_inc(mid_hi_ready, 1)

        @block.vector
        def _(dve):
            def add_out(n, b, banks=None):
                dve.wait_ge(out_done, B * n + b + 1)
                of = (banks or VO * HALF)[b]
                dve.tensor_tensor(acc[:, b, :], of[:, :], acc[:, b, :], ALU.add).then_inc(out_added, 1)

            def row_stats(layer, b):
                if layer == 0:
                    dve.wait_ge(x_loaded[b], 16)
                else:
                    dve.wait_ge(out_added, (0, 0, B * GROUPS)[layer] + b + 1)
                dve.bn_stats(stats[:, b, :], acc[:, b, :]).then_inc(stats_step, 1)

            spread_steps = [0]

            def spread_chained(ins):
                spread_steps[0] += 1
                ins.then_inc(spread_step, 1)
                dve.wait_ge(spread_step, spread_steps[0])

            def spreads(layer, h):
                var = mean_var[:, h, 1]
                dve.wait_ge(stats_step, B * layer + h.stop)
                for b in range(h.start, h.stop):
                    ins = dve.bn_aggr(mean_var[:, b, :], stats[:, b, :])
                spread_chained(ins)
                dve.tensor_scalar(neg_mean[:, h], mean_var[:, h, 0], -1.0, None, ALU.mult)
                ins = dve.tensor_scalar(spread[:, 0, h], var, EPS, None, ALU.add)
                if layer == 1:
                    spread_chained(ins)
                    spread_chained(dve.reciprocal(spread[:, 1, h], spread[:, 0, h]))
                    spread_chained(dve.tensor_tensor(spread[:, 1, h], spread[:, 1, h], var, ALU.mult))
                    ins = dve.tensor_scalar(spread[:, 1, h], spread[:, 1, h], EPS, None, ALU.add)
                ins.then_inc(spread_ready, 1)

            def normalise(h, count):
                dve.wait_ge(rstd_ready, count)
                for b in range(h.start, h.stop):
                    ins = dve.tensor_scalar(rows[:, b, :], acc[:, b, :], mean_var[:, b, 0:1], rstd[:, 0, b:b + 1],
                                            ALU.subtract, ALU.mult)
                ins.then_inc(rows_ready, 1)

            def normalise_both(b):
                dve.wait_ge(rstd_ready, spans(1, 1))
                return dve.tensor_scalar(rows[:, b, :], acc[:, b, :], rstd_rms[:, b:b + 1], shift[:, b:b + 1],
                                         ALU.mult, ALU.add)

            def add_normalised(i):
                h = half(i)
                dve.wait_ge(rstd_ready, spans(1, i))
                dve.tensor_scalar(gain[:, h], rstd[:, 0, h], 1.0, None, ALU.add)
                dve.tensor_tensor(offset[:, h], neg_mean[:, h], rstd[:, 0, h], ALU.mult).then_inc(norm_step, 1)
                dve.wait_ge(norm_step, i + 1)
                dve.wait_ge(rows_ready, spans(1, i))
                for b in range(HALF * i, HALF * (i + 1)):
                    ins = dve.tensor_scalar(acc[:, b, :], acc[:, b, :], gain[:, b:b + 1], offset[:, b:b + 1],
                                            ALU.mult, ALU.add)
                ins.then_inc(residual_added, 1)

            def split_rows(layer, i, chunks=range(KC)):
                for c in chunks:
                    n = KC * i + c
                    dve.wait_ge(xt_hi_ready, 2 * KC * layer + n + 1)
                    of, hi = ROWS_T[layer][c][:, :], xt[0][:, c, cols(i, BANK)].bitcast(F32)
                    to = xt[1][:, c, cols(i, BANK)]
                    if layer == 1:
                        ins = dve.scalar_tensor_tensor(out=to, in0=of, scalar=ln_w_cols[:, c:c + 1], in1=hi,
                                                       op0=ALU.mult, op1=ALU.subtract)
                    else:
                        ins = dve.tensor_tensor(to, of, hi, ALU.subtract)
                    ins.then_inc(xt_lo_ready, 1)

            def take_scores(s, i, add=True):
                dve.wait_ge(scores_done, 2 * s + i + 1)
                if add:
                    if i == 0:
                        dve.wait_ge(bias_mask_ready, s)
                    ins = dve.tensor_tensor(probs[:, half(i), :], tiles(SC[i]), bias_mask[:, half(i), :], ALU.add)
                else:
                    ins = dve.tensor_scalar(probs[:, half(i), :], tiles(SC[i]), SCORE_SCALE, None, ALU.mult)
                ins.then_inc(scores_biased, 1)

            def maxima(s, i):
                dve.wait_ge(scores_biased, 2 * s + i + 1)
                dve.tensor_reduce(neg_max[:, half(i)], probs[:, half(i), :], AX.X, ALU.max,
                                  negate=True).then_inc(max_ready, 1)

            def normalise_probs(s, i, masked=True):
                dve.wait_ge(exp_done, 2 * s + i + 1)
                dve.reciprocal(inv[:, half(i)], sums[:, half(i)]).then_inc(inv_ready, 1)
                dve.wait_ge(inv_ready, 2 * s + i + 1)
                scale = inv
                if masked:
                    dve.tensor_tensor(row_scale[:, half(i)], inv[:, half(i)], has_key[:, half(i)],
                                      ALU.mult).then_inc(scale_ready, 1)
                    dve.wait_ge(scale_ready, 2 * s - 2 + i + 1)
                    scale = row_scale
                dve.tensor_tensor(probs[:, half(i), :], probs[:, half(i), :],
                                  scale[:, half(i)].unsqueeze(2).to_broadcast([P, HALF, P]),
                                  ALU.mult).then_inc(probs_ready, 1)

            def copy_probs_t(s):
                dve.wait_ge(probs_turned, 2 * s + 2)
                dve.tensor_copy(probs_t[:, half(1), :], tiles(TO[1])).then_inc(probs_t1_copied, 1)

            def split_out(s, j, halves=(0, 1), to=ot):
                for i in halves:
                    dve.wait_ge(ot_hi_ready, 2 * s + i + 1)
                    c = cols(2 * j + i, BANK)
                    dve.tensor_tensor(to[1][:, c], TO[i][:, :], to[0][:, c].bitcast(F32),
                                      ALU.subtract).then_inc(ot_lo_ready, 1)

            def split_weights(piece, g, to=None):
                to = piece if to is None else to
                dve.wait_ge(w_hi_ready[piece], g + 1)
                dve.tensor_tensor(w[1][:, to, :], raw[:, piece, :], w[0][:, to, :].bitcast(F32),
                                  ALU.subtract).then_inc(w_lo_ready[piece], 1)

            def group(g, last=False):
                normalise_probs(PAIR * g, 0)
                normalise_probs(PAIR * g, 1)
                split_weights(QKB, g)
                copy_probs_t(PAIR * g)
                for i in range(2):
                    take_scores(PAIR * g + 1, i)
                for i in range(2):
                    maxima(PAIR * g + 1, i)
                split_out(PAIR * g, 1)
                for i in range(2):
                    normalise_probs(PAIR * g + 1, i)
                if last:
                    split_weights(WO, g, WO_LAST)
                else:
                    split_weights(QKA, g + 1)
                copy_probs_t(PAIR * g + 1)
                if last:
                    for i in range(2):
                        take_scores(HEADS, i)
                    for i in range(2):
                        maxima(HEADS, i)
                for b in range(B):
                    if last and b in (2, 5):
                        normalise_probs(HEADS, b // 4)
                    if last and b in (4, 7):
                        split_out(PAIR * g + 1, 0, (b // 7,), to=ot_last)
                    add_out(g, b)
                if not last:
                    split_weights(WV, g + 1)
                    split_weights(WO, g)
                    split_out(PAIR * g + 1, 0)
                    for i in range(2):
                        take_scores(PAIR * g + 2, i)
                    for i in range(2):
                        maxima(PAIR * g + 2, i)

            for k in range(2):
                span = slice(2 * k, 2 * k + 2)
                for b in (2 * k, 2 * k + 1):
                    row_stats(0, b)
                spreads(0, span)
            for k in range(2):
                normalise(slice(2 * k, 2 * k + 2), k + 1)
            dve.wait_ge(w_qkv_hi_ready, 1)
            dve.tensor_tensor(ot[1][:, QKV_COLS], raw_a[:, QKV_COLS], ot[0][:, QKV_COLS].bitcast(F32),
                              ALU.subtract).then_inc(w_qkv_lo_ready, 1)
            split_rows(0, 0)
            for b in range(HALF, B):
                row_stats(0, b)
            spreads(0, half(1))
            normalise(half(1), spans(0, 1))
            split_rows(0, 1)

            def copy_values(i):
                dve.wait_ge(values_turned, i + 1)
                dve.tensor_copy(vt_tiles[:, cols(i, BANK)], VO[i][:, :]).then_inc(values_copied, 1)

            def add_b_o(i):
                if i == 0:
                    dve.wait_ge(small_loaded, 48)
                for b in range(HALF * i, HALF * (i + 1)):
                    dve.tensor_tensor(acc[:, b, :], acc[:, b, :], b_o_rows, ALU.add).then_inc(bo_added, 1)

            take_scores(0, 0, add=False)
            maxima(0, 0)
            copy_values(0)
            add_b_o(0)
            normalise_probs(0, 0, masked=False)
            split_weights(QKA, 0)
            take_scores(0, 1, add=False)
            maxima(0, 1)
            copy_values(1)
            split_weights(WV, 0)
            normalise_probs(0, 1, masked=False)
            split_out(0, 0, (0,))
            copy_probs_t(0)
            dve.wait_ge(bo_added, HALF)
            for b in range(HALF):
                add_out(0, b, OWN_OUT)
            add_b_o(1)
            split_out(0, 0, (1,))
            for b in range(HALF):
                row_stats(1, b)
            spreads(1, half(0))
            dve.wait_ge(bo_added, B)
            for b in range(HALF, B):
                add_out(0, b, OWN_OUT)
            for b in range(HALF, B):
                row_stats(1, b)
            spreads(1, half(1))
            add_normalised(0)
            split_rows(1, 0, (0,))
            normalise_both(4)
            split_rows(1, 0, (1, 2))
            normalise_both(5).then_inc(rows_ready_v, 1)
            split_rows(1, 0, (3,))
            split_weights(QKB, 0)
            split_rows(1, 1)
            dve.wait_ge(mask_loaded, 16)
            dve.tensor_scalar(mask_add[:, :, :], mask_raw[:, :, :], -1.0, -MASKED, ALU.add,
                              ALU.mult).then_inc(mask_ready, 1)
            dve.tensor_reduce(has_key[:, :], mask_raw[:, :, :], AX.X, ALU.max).then_inc(mask_step, 1)
            for i in range(2):
                take_scores(1, i)
            for i in range(2):
                maxima(1, i)
            split_weights(WV, 1)
            dve.wait_ge(mask_step, 1)
            for i in range(2):
                normalise_probs(1, i)
            split_weights(QKA, 1)
            add_normalised(1)
            copy_probs_t(1)
            split_out(1, 0)
            for i in range(2):
                take_scores(2, i)
            for i in range(2):
                maxima(2, i)
            split_weights(WO, 0)
            dve.wait_ge(residual_added, 2)
            with dve.Fori(1, GROUPS - 1) as g:
                group(g)
            group(GROUPS - 1, last=True)
            copy_probs_t(HEADS)
            split_out(HEADS, 1, to=ot_last)
            def normalise_last(i):
                dve.wait_ge(ffn_lo_ready, 1)
                dve.wait_ge(rstd_ready, spans(2, i))
                for b in range(HALF * i + HALF // 2, HALF * (i + 1)):
                    ins = dve.tensor_scalar(rows[:, b, :], acc[:, b, :], mean_var[:, b, 0:1], rstd[:, 0, b:b + 1],
                                            ALU.subtract, ALU.mult)
                ins.then_inc(rows_ready_v, 1)

            for b in range(HALF):
                add_out(GROUPS, b, LAST_OUT)
                if b:
                    row_stats(2, b - 1)
            row_stats(2, HALF - 1)
            spreads(2, half(0))
            add_out(GROUPS, 4, LAST_OUT)
            add_out(GROUPS, 5, LAST_OUT)
            normalise_last(0)
            add_out(GROUPS, 6, LAST_OUT)
            add_out(GROUPS, 7, LAST_OUT)
            row_stats(2, 4)
            split_rows(2, 0)
            for b in (5, 6, 7):
                row_stats(2, b)
            spreads(2, half(1))
            normalise_last(1)
            split_rows(2, 1)
            steps = [0]

            def chained(ins):
                steps[0] += 1
                ins.then_inc(route_step, 1)
                dve.wait_ge(route_step, steps[0])

            def route(i):
                h = half(i)
                dve.wait_ge(routed_done, 2 * (i + 1))
                for n in range(2):
                    tile_pair = VO[n][:, :].rearrange("p (t n) -> p t n", t=2)[:, :, NE * NR:NE * NR + NE]
                    ins = dve.tensor_copy(rank[:, h, :].rearrange("p (t n) e -> p n t e", n=2)[:, n], tile_pair)
                    chained(ins)
                chained(dve.tensor_reduce(top[:, h], rank[:, h, :], AX.X, ALU.max))
                dve.tensor_tensor(logits[:, h, :], rank[:, h, :], top[:, h].unsqueeze(2).to_broadcast([P, HALF, NE]),
                                  ALU.subtract).then_inc(logits_ready, 1)
                dve.wait_ge(gates_exp, i + 1)
                flat = gates[:, h, :].rearrange("p t e -> p (t e)")
                others = gates[:, h, :].unsqueeze(2).to_broadcast([P, HALF, NE, NE])
                own = flat.unsqueeze(2).to_broadcast([P, HALF * NE, NE]).rearrange("p (t e) j -> p t e j", e=NE)
                beats4 = beats[:, :, :].rearrange("p (t e) j -> p t e j", e=NE)
                ties4 = ties[:, :, :].rearrange("p (t e) j -> p t e j", e=NE)
                before = earlier[:, :, :].unsqueeze(1).to_broadcast([P, HALF, NE, NE])
                chained(dve.tensor_tensor(beats4, others, own, ALU.is_gt))
                chained(dve.tensor_tensor(ties4, others, own, ALU.is_equal))
                chained(dve.tensor_tensor(ties4, ties4, before, ALU.mult))
                chained(dve.tensor_tensor(beats[:, :, :], beats[:, :, :], ties[:, :, :], ALU.add))
                chained(dve.tensor_reduce(rank[:, h, :].rearrange("p t e -> p (t e)"), beats[:, :, :], AX.X, ALU.add))
                chained(dve.scalar_tensor_tensor(out=logits[:, h, :], in0=rank[:, h, :], scalar=1.5,
                                                 in1=gates[:, h, :], op0=ALU.is_lt, op1=ALU.mult))
                chained(dve.tensor_reduce(top_sum[:, h], logits[:, h, :], AX.X, ALU.add))
                chained(dve.reciprocal(top[:, h], top_sum[:, h]))
                chained(dve.scalar_tensor_tensor(out=rank[:, h, :], in0=logits[:, h, :], scalar=LORA_SCALE,
                                                 in1=top[:, h].unsqueeze(2).to_broadcast([P, HALF, NE]),
                                                 op0=ALU.mult, op1=ALU.mult))
                for t in range(HALF):
                    b = HALF * i + t
                    at = ROUTED * (t // 2)
                    mids = VO[t % 2][:, at:at + NE * NR].rearrange("p (e r) -> p e r", e=NE)
                    ins = dve.tensor_tensor(probs[:, b, :].rearrange("p (e r) -> p e r", e=NE), mids,
                                            rank[:, b, :].unsqueeze(2).to_broadcast([P, NE, NR]), ALU.mult)
                ins.then_inc(mid_ready, 1)

            def split_mid(i):
                dve.wait_ge(mid_hi_ready, i + 1)
                dve.tensor_tensor(ot[1][:, cols(i, BANK)], TO[i][:, :], ot[0][:, cols(i, BANK)].bitcast(F32),
                                  ALU.subtract).then_inc(mid_lo_ready, 1)

            def results(i):
                for t in range(HALF):
                    b = HALF * i + t
                    dve.wait_ge(ffn_done, b + 1)
                    dve.tensor_tensor(acc[:, b, :], BASE[t][:, :], acc[:, b, :], ALU.add).then_inc(result_ready, 1)

            dve.wait_ge(consts_ready, 1)
            route(0)
            split_mid(0)
            results(0)
            route(1)
            split_mid(1)
            results(1)


def kernel(x, ctx_4096, mask_BxSxS2_bk0, L0_attn_Wqkv, L0_attn_bqkv, L0_attn_Wo, L0_attn_bo,
           L0_xattn_position_bias, L0_xattn_ln_weight, L0_xattn_w_q, L0_xattn_w_k, L0_xattn_w_v, L0_xattn_w_out,
           L0_ffn_base_W, L0_ffn_router_W, L0_ffn_lora_A, L0_ffn_lora_B):
    import numpy as np
    import concourse.bacc as bacc
    from concourse.bass_utils import run_bass_kernel_spmd

    def chunked(a):
        a = np.asarray(a)
        return a.reshape(KC, P, a.shape[1]).transpose(1, 0, 2).reshape(P, KC * a.shape[1])

    f = np.float32
    q, k, v = (np.asarray(a).reshape(GROUPS, PAIR, P, KC, P) for a in (L0_xattn_w_q, L0_xattn_w_k, L0_xattn_w_v))
    pieces = np.empty((GROUPS, 4, P, PIECE), f)
    for j, piece in ((0, QKA), (1, QKB)):
        pieces[:, piece] = np.stack([a[:, j].transpose(0, 3, 2, 1) for a in (q, k)], axis=2).reshape(GROUPS, P, PIECE)
    pieces[:, WV] = v.transpose(0, 4, 3, 1, 2).reshape(GROUPS, P, PIECE)
    pieces[:, WO] = np.asarray(L0_xattn_w_out).T.reshape(GROUPS, PAIR, P, C).transpose(0, 2, 1, 3).reshape(
        GROUPS, P, PIECE)
    routed = np.zeros((C, ROUTED), f)
    routed[:, 0:NE * NR] = np.asarray(L0_ffn_lora_A).transpose(1, 0, 2).reshape(C, NE * NR)
    routed[:, NE * NR:NE * NR + NE] = np.asarray(L0_ffn_router_W).T
    arrays = {
        "x": np.asarray(x).transpose(1, 0, 2),
        "ctx_t": np.asarray(ctx_4096).reshape(T, KC, P).transpose(2, 1, 0),
        "mask": np.asarray(mask_BxSxS2_bk0).transpose(1, 0, 2),
        "w_qkv": chunked(L0_attn_Wqkv),
        "b_qkv": np.asarray(L0_attn_bqkv).reshape(3, P).T,
        "w_o": np.asarray(L0_attn_Wo),
        "b_o": np.asarray(L0_attn_bo),
        "ln_w": np.asarray(L0_xattn_ln_weight).reshape(KC, P).T,
        "pos_bias": np.asarray(L0_xattn_position_bias).reshape(GROUPS, PAIR, P, P).transpose(0, 2, 1, 3),
        "weights": pieces,
        "w_base": chunked(np.asarray(L0_ffn_base_W).T),
        "w_routed": chunked(routed),
        "w_lora_b": np.asarray(L0_ffn_lora_B).reshape(NE * NR, C),
    }
    nc = bacc.Bacc("TRN2", target_bir_lowering=False, num_devices=1)
    sent, args = {}, []
    for name, a in arrays.items():
        a = np.ascontiguousarray(a)
        sent[f"in_{name}"] = a
        args.append(nc.dram_tensor(f"in_{name}", a.shape, mybir.dt.from_np(a.dtype), kind="ExternalInput").ap())
    args.append(nc.dram_tensor("out_rows", (P, B, C), F32, kind="ExternalOutput").ap())
    decoder_kernel(nc, *args)
    result = run_bass_kernel_spmd(nc, [sent], core_ids=[0])
    return np.ascontiguousarray(result.results[0]["out_rows"].transpose(1, 0, 2))
```
